# Optimizing a Trainium2 kernel written in Bass

```python
import numpy as np
import jax
import jax.numpy as jnp

def _softmax(x, axis=-1):
    return jax.nn.softmax(x, axis=axis)

def _gelu(x):
    return jax.nn.gelu(x, approximate=True)

def _silu(x):
    return jax.nn.silu(x)

def _sigmoid(x):
    return jax.nn.sigmoid(x)

def _layernorm(x, axis=-1, eps=1e-05):
    m = jnp.mean(x, axis=axis, keepdims=True)
    v = jnp.var(x, axis=axis, keepdims=True)
    return (x - m) / jnp.sqrt(v + eps)

def _scatter_add(tgt, idx, src, axis=0):
    return tgt.at[idx].add(src)

def _segment_sum(src, seg, n):
    return jax.ops.segment_sum(src, seg, n)
kernel_name = 'mk_gnn_resnorm_d1_gnn_r64_7f7786'

def setup_inputs(seed: int=0):
    np.random.seed(seed)
    _w = jnp.asarray

    def _rec_inputs():
        import jax
        import jax.numpy as jnp
        _gk = jax.random.key(seed)
        x = -1.686e-05 + 1 * jax.random.normal(jax.random.fold_in(_gk, 1), (50000, 160), jnp.float32)
        src = jax.random.randint(jax.random.fold_in(_gk, 2), (25000,), 0, 50000, jnp.int32)
        dst = jnp.minimum((50000 * jax.random.uniform(jax.random.fold_in(_gk, 3), (25000,)) ** 2.0).astype(jnp.int32), 49999)
        _o = jnp.argsort(dst, stable=True)
        src = src[_o]
        dst = dst[_o]
        edge_attr_4 = 0.0007022 + 0.999661 * jax.random.normal(jax.random.fold_in(_gk, 11), (25000, 4), jnp.float32)
        node_vec1 = -0.00915711 + 0.999674 * jax.random.normal(jax.random.fold_in(_gk, 13), (50000, 1), jnp.float32)
        return (x, src, dst, edge_attr_4, node_vec1)
    x, src, dst, edge_attr_4, node_vec1 = _rec_inputs()

    def _L0_gnn_setup():
        import jax, jax.numpy as jnp
        import numpy as np
        MUL0, MUL1 = (64, 32)
        INV_SQRT3 = 1.0 / np.sqrt(3.0)

        def _split(x):
            return (x[:, :MUL0], x[:, MUL0:].reshape(x.shape[0], MUL1, 3))

        def _merge(o0, o1):
            return jnp.concatenate([o0, o1.reshape(o1.shape[0], -1)], axis=-1)

        def _tp(x0, x1, y0, y1, w000, w011, w101, w110):
            fan0 = x0.shape[1] * y0.shape[1] + x1.shape[1] * y1.shape[1]
            fan1 = x0.shape[1] * y1.shape[1] + x1.shape[1] * y0.shape[1]
            out0 = (jnp.einsum('eu,ev,uvw->ew', x0, y0, w000) + INV_SQRT3 * jnp.einsum('euk,evk,uvw->ew', x1, y1, w110)) / np.sqrt(fan0)
            out1 = (jnp.einsum('eu,evk,uvw->ewk', x0, y1, w011) + jnp.einsum('euk,ev,uvw->ewk', x1, y0, w101)) / np.sqrt(fan1)
            return (out0, out1)

        def _lin(x0, x1, w0, w1):
            return (x0 @ w0 / np.sqrt(x0.shape[1]), jnp.einsum('euk,uv->evk', x1, w1) / np.sqrt(x1.shape[1]))
        key = jax.random.key(seed)
        ks = jax.random.split(key, 20)
        N, E = (50000, 500000)
        inp = {'node_features': jax.random.normal(ks[0], (N, MUL0 + 3 * MUL1), dtype=jnp.float32), 'edge_index': jax.random.randint(ks[1], (2, E), 0, N, dtype=jnp.int64), 'edge_attr_tensor': jax.random.normal(ks[2], (E, 4), dtype=jnp.float32), 'node_attr_scalar_raw': jax.random.normal(ks[3], (N, 1), dtype=jnp.float32), 'wm000': jax.random.normal(ks[4], (MUL0, 1, MUL0), dtype=jnp.float32), 'wm011': jax.random.normal(ks[5], (MUL0, 1, MUL1), dtype=jnp.float32), 'wm101': jax.random.normal(ks[6], (MUL1, 1, MUL1), dtype=jnp.float32), 'wm110': jax.random.normal(ks[7], (MUL1, 1, MUL0), dtype=jnp.float32), 'lm0': jax.random.normal(ks[8], (MUL0, MUL0), dtype=jnp.float32), 'lm1': jax.random.normal(ks[9], (MUL1, MUL1), dtype=jnp.float32), 'wu000': jax.random.normal(ks[10], (MUL0, MUL0, MUL0), dtype=jnp.float32), 'wu011': jax.random.normal(ks[11], (MUL0, MUL1, MUL1), dtype=jnp.float32), 'wu101': jax.random.normal(ks[12], (MUL1, MUL0, MUL1), dtype=jnp.float32), 'wu110': jax.random.normal(ks[13], (MUL1, MUL1, MUL0), dtype=jnp.float32), 'lu0': jax.random.normal(ks[14], (MUL0, MUL0), dtype=jnp.float32), 'lu1': jax.random.normal(ks[15], (MUL1, MUL1), dtype=jnp.float32)}
        return inp
    _L0_gnn_all = _L0_gnn_setup()
    _L0_gnn_in = {k: v for k, v in _L0_gnn_all.items() if k in ('wm000', 'wm011', 'wm101', 'wm110', 'lm0', 'lm1', 'wu000', 'wu011', 'wu101', 'wu110', 'lu0', 'lu1')}
    del _L0_gnn_all
    return {'x': x, 'src': src, 'dst': dst, 'edge_attr_4': edge_attr_4, 'node_vec1': node_vec1, 'L0_gnn_wm000': _L0_gnn_in['wm000'], 'L0_gnn_wm011': _L0_gnn_in['wm011'], 'L0_gnn_wm101': _L0_gnn_in['wm101'], 'L0_gnn_wm110': _L0_gnn_in['wm110'], 'L0_gnn_lm0': _L0_gnn_in['lm0'], 'L0_gnn_lm1': _L0_gnn_in['lm1'], 'L0_gnn_wu000': _L0_gnn_in['wu000'], 'L0_gnn_wu011': _L0_gnn_in['wu011'], 'L0_gnn_wu101': _L0_gnn_in['wu101'], 'L0_gnn_wu110': _L0_gnn_in['wu110'], 'L0_gnn_lu0': _L0_gnn_in['lu0'], 'L0_gnn_lu1': _L0_gnn_in['lu1']}

def reference(x, src, dst, edge_attr_4, node_vec1, L0_gnn_wm000, L0_gnn_wm011, L0_gnn_wm101, L0_gnn_wm110, L0_gnn_lm0, L0_gnn_lm1, L0_gnn_wu000, L0_gnn_wu011, L0_gnn_wu101, L0_gnn_wu110, L0_gnn_lu0, L0_gnn_lu1):
    import jax
    import jax.numpy as jnp

    def _L0_gnn_ref(node_features, edge_index, edge_attr_tensor, node_attr_scalar_raw, wm000, wm011, wm101, wm110, lm0, lm1, wu000, wu011, wu101, wu110, lu0, lu1):
        import jax, jax.numpy as jnp
        import numpy as np
        MUL0, MUL1 = (64, 32)
        INV_SQRT3 = 1.0 / np.sqrt(3.0)

        def _split(x):
            return (x[:, :MUL0], x[:, MUL0:].reshape(x.shape[0], MUL1, 3))

        def _merge(o0, o1):
            return jnp.concatenate([o0, o1.reshape(o1.shape[0], -1)], axis=-1)

        def _tp(x0, x1, y0, y1, w000, w011, w101, w110):
            fan0 = x0.shape[1] * y0.shape[1] + x1.shape[1] * y1.shape[1]
            fan1 = x0.shape[1] * y1.shape[1] + x1.shape[1] * y0.shape[1]
            out0 = (jnp.einsum('eu,ev,uvw->ew', x0, y0, w000) + INV_SQRT3 * jnp.einsum('euk,evk,uvw->ew', x1, y1, w110)) / np.sqrt(fan0)
            out1 = (jnp.einsum('eu,evk,uvw->ewk', x0, y1, w011) + jnp.einsum('euk,ev,uvw->ewk', x1, y0, w101)) / np.sqrt(fan1)
            return (out0, out1)

        def _lin(x0, x1, w0, w1):
            return (x0 @ w0 / np.sqrt(x0.shape[1]), jnp.einsum('euk,uv->evk', x1, w1) / np.sqrt(x1.shape[1]))
        N = node_features.shape[0]
        row, col = (edge_index[0], edge_index[1])
        r_vec = edge_attr_tensor[:, :3]
        dist = edge_attr_tensor[:, 3:4]
        e0 = dist
        e1 = r_vec[:, None, :]
        xj0, xj1 = _split(node_features[col])
        m0, m1 = _tp(xj0, xj1, e0, e1, wm000, wm011, wm101, wm110)
        d0, d1 = _lin(xj0, xj1, lm0, lm1)
        msgs = _merge(m0 + d0, m1 + d1)
        agg = jax.ops.segment_sum(msgs, row, num_segments=N)
        a0, a1 = _split(agg)
        x0, x1 = _split(node_features)
        u0, u1 = _tp(x0, x1, a0, a1, wu000, wu011, wu101, wu110)
        ud0, ud1 = _lin(x0, x1, lu0, lu1)
        return node_features + _merge(u0 + ud0, u1 + ud1)
    edge_index = jnp.stack([src, dst])
    x = _layernorm(x + _L0_gnn_ref(x, edge_index, edge_attr_4, node_vec1, L0_gnn_wm000, L0_gnn_wm011, L0_gnn_wm101, L0_gnn_wm110, L0_gnn_lm0, L0_gnn_lm1, L0_gnn_wu000, L0_gnn_wu011, L0_gnn_wu101, L0_gnn_wu110, L0_gnn_lu0, L0_gnn_lu1), axis=-1)
    return x

_drawn_inputs = setup_inputs


def setup_inputs(seed=0):
    import zlib

    import numpy as np

    out = dict(_drawn_inputs(seed))
    spreads = {}
    factors = {}
    for name, (base, spread) in spreads.items():
        noise = np.random.default_rng([zlib.crc32(name.encode()), seed]).standard_normal(out[name].shape)
        drawn = base * np.exp(spread * noise) if base else spread * noise
        out[name] = jnp.asarray(drawn.astype(out[name].dtype))
    for name, factor in factors.items():
        out[name] = (out[name] * factor).astype(out[name].dtype)
    return out
```

```python
import concourse.bass as bass
from concourse import mybir
from contextlib import ExitStack
import numpy as np

N, E, F0, F1, C = 50000, 25000, 64, 32, 160
P = 125
J = 4
T = P * J
TILES = E // T
COLS = E // P
NT = N // T
NA = F0 // 2
GA = NA // 4
GB = F1 // 4
DUMP = P
ZR = 10
EPS = 1e-5

SEL2, SEL4, REP4, REPA, STK = 0, 16, 24, 25, 27
NSEL = 31


def selectors():
    k = np.arange(96)[:, None] % 32
    m = np.arange(128)[None, :]
    parts = [k == 2 * c + m // 64 for c in range(16)]
    parts += [k == 4 * c + m // 32 for c in range(8)]
    parts += [k == m % 32]
    parts += [k + 32 * b == m % 64 for b in range(2)]
    parts += [(k == m % 32) & (m // 32 == q) for q in range(4)]
    return np.concatenate([np.broadcast_to(a, (96, 128)) for a in parts], 1)


def constants():
    p = np.arange(128)
    vec = np.arange(96)
    perm = np.eye(96)
    return {
        "c_sel": (selectors(), "bfloat16"),
        "c_eyeb": (np.eye(128), "bfloat16"),
        "c_eye": (np.eye(128), "float32"),
        "c_fold": (p[:, None] % 64 == np.arange(64)[None, :], "float32"),
        "c_sum4": (p[:, None] % 32 == np.arange(32)[None, :], "float32"),
        "c_earlier": (np.arange(P)[None, :] < np.arange(P)[:, None], "float32"),
        "c_dump": (N + np.arange(P)[:, None], "float32"),
    }


BACK_AT = {2: ["ul0", "ul1"], 3: ["ud0", "ud1"]}
FRONT_AT = {9: ["ft0", "ft1", "ft2"], 10: ["m0", "m1"], 11: [f"sx{b}" for b in range(5)],
            13: [f"sa{b}" for b in range(5)], 14: [f"rep{r}" for r in range(5)]}
FRONT = [a for s in sorted(FRONT_AT) for a in FRONT_AT[s]]


def aux_order(back, front):
    order = []
    for s in range(16):
        if back:
            order += BACK_AT.get(s, [])
        if s >= GA:
            order += [f"t101_{s - GA}", f"t011_{s - GA}"]
        if front:
            order += FRONT_AT.get(s, [])
    return order


NAUX = len(aux_order(True, True))
NBACK = 4
assert NAUX % 2 == 0 and len(FRONT) == 20


def aux_base(t):
    return t * NAUX + len(FRONT) - NBACK


class Pos:

    def __init__(self, t, back, front):
        order = aux_order(back, front)
        self.start = 0 if back else NBACK
        self.base = aux_base(t)
        self.at = {a: self.start + n for n, a in enumerate(order)}

    def bank(self, name):
        return (self.at[name] + len(FRONT) - NBACK) % 2

    def after(self, name):
        return self.base + (self.at[name] + 1)


class ProloguePos:
    def __init__(self):
        self.at = {a: n for n, a in enumerate(FRONT)}

    def bank(self, name):
        return self.at[name] % 2

    def after(self, name):
        return self.at[name] + 1


class TailPos:

    def __init__(self):
        first = aux_base(TILES - 1) + len(aux_order(True, False))
        self.at = {a: first + n for n, a in enumerate(["ul0", "ul1", "ud0", "ud1"])}

    def bank(self, name):
        return self.at[name] % 2

    def after(self, name):
        return self.at[name] + 1


NV = 3 * GA + 9 * GB


def v_a(g, i):
    return 3 * g + i


def v_bc(c, k, which):
    return 3 * GA + 9 * c + 3 * k + which


NX = 4 * GA + 6 * GB


def occupant_done(n):
    if n < 4 * GA:
        g, i = divmod(n, 4)
        return ("v", v_a(g, i) + 1) if i < 3 else ("s", g + 1)
    c, r = divmod(n - 4 * GA, 6)
    k, a = divmod(r, 2)
    return ("v", v_bc(c, k, 1 + a) + 1)


def build(nc, x, xT, src, srcT, dst, attr, wm000, wm011, wm101, wm110, lm0, lm1, wu000, wu011, wu101, wu110,
          lu0, lu1, c_sel, c_eyeb, c_eye, c_fold, c_sum4, c_earlier, c_dump, out):
    f32, b16, i32 = mybir.dt.float32, mybir.dt.bfloat16, mybir.dt.int32
    ALU, ACT, AX = mybir.AluOpType, mybir.ActivationFunctionType, mybir.AxisListType
    ctx = ExitStack()
    with ctx:
        def sb(name, shape, dt=f32):
            return ctx.enter_context(nc.sbuf_tensor(name, shape, dt))

        def sem(name):
            return ctx.enter_context(nc.semaphore(name))

        acc = nc.dram_tensor("acc", (N + DUMP, C), f32, kind="Internal").ap()

        sel = sb("sel", [96, NSEL, 128], b16)
        eyeb = sb("eyeb", [128, 128], b16)
        eye = sb("eye", [128, 128])
        fold = sb("fold", [128, 64])
        sum4 = sb("sum4", [128, 32])
        earlier = sb("earlier", [P, P])
        dump = sb("dump", [P, 1])
        zeros = sb("zeros", [P, ZR * C])
        w000 = sb("w000", [128, NA, F0])
        w110 = sb("w110", [128, GB, F0])
        wt = sb("wt", [128, 2 * GB, 128])
        wa = sb("wa", [128, C + F1])
        wb = sb("wb", [96, 96])
        wc = sb("wc", [128, C])
        wl0 = sb("wl0", [128, C])
        wl1 = sb("wl1", [128, C])
        src_all = sb("src_all", [P, COLS], i32)
        dst_all = sb("dst_all", [P, COLS], i32)
        attr_all = sb("attr_all", [P, COLS * 4])
        dcur = sb("dcur", [P, J], i32)
        scur = sb("scur", [P, J], i32)
        acur = sb("acur", [P, J, 4])
        G = sb("G", [P, J, F0 + C])
        H = sb("H", [P, J, 128])
        rx1 = sb("rx1", [P, J, 3, F1])
        XI = sb("XI", [P, J, C])
        M = sb("M", [P, J, C + F1])
        rz = sb("rz", [P, J, 3, F1])
        RX = sb("RX", [P, J, C])
        RA = sb("RA", [P, J, C])
        SX = sb("SX", [P, J, 5, 3, 32], b16)
        SA = sb("SA", [P, J, 5, 3, 32], b16)
        FT = sb("FT", [128, 3, T])
        ST = sb("ST", [96, 2, 10, T], b16)
        REP = sb("REP", [128, 2, 5, T])
        arena = sb("arena", [128, 30, T])
        PA = arena[:, 0:8, :]
        PB = arena[:, 8:14, :].rearrange("p (g k) e -> p g k e", g=2)
        ZB = arena[:, 14:20, :].rearrange("p (g k) e -> p g k e", g=2)
        ZC = arena[:, 20:26, :].rearrange("p (g k) e -> p g k e", g=2)
        TS = arena[:, 26:30, :]
        QB = sb("QB", [128, 2, T])
        XS = sb("XS", [128, 2, T])
        U0 = sb("U0", [128, T])
        U1 = sb("U1", [96, T])
        UL = sb("UL", [P, J, C])
        UD = sb("UD", [P, J, C])
        rows = sb("rows", [P, J, P], i32)
        srcf = sb("srcf", [P, J])
        same = sb("same", [P, J, P])
        prior = sb("prior", [P, J, P])
        dup = sb("dup", [P, J])
        todump = sb("todump", [P, J])
        sidx = sb("sidx", [P, J], i32)
        xa = arena[:, 0:3, :]
        xb = arena[:, 3:6, :]
        ya = arena[0:P, 6:14, :].rearrange("p n e -> p (n e)")[:, 0:3 * J * C].rearrange("p (b f) -> p b f", b=3)
        yo = arena[0:P, 14:22, :].rearrange("p n e -> p (n e)")[:, 0:3 * J * C].rearrange("p (b f) -> p b f", b=3)
        stats = sb("stats", [P, 3, J, 6])
        mv = sb("mv", [P, 3, J, 2])
        ve, sd, r0, hv, rs, nb = (sb(n, [P, 3, J]) for n in ("ve", "sd", "r0", "hv", "rs", "nb"))

        copies = [ctx.enter_context(nc.psum_tensor(f"copies{b}", [128, 512], f32)) for b in range(4)]
        acc0 = ctx.enter_context(nc.psum_tensor("acc0", [128, 512], f32))
        acc1 = ctx.enter_context(nc.psum_tensor("acc1", [128, 512], f32))
        pairs = [copies[0:2], copies[2:4], [acc0, acc1]]
        aux = [ctx.enter_context(nc.psum_tensor(f"aux{b}", [128, 512], f32)) for b in range(2)]

        consts_in = sem("consts_in")
        weights_in = sem("weights_in")
        tables_in = sem("tables_in")
        small_zeroed = sem("small_zeroed")
        zeros_made = sem("zeros_made")
        acc_zeroed = sem("acc_zeroed")
        weights_ready = sem("weights_ready")
        wl_ready = sem("wl_ready")
        idx_cur = sem("idx_cur")
        parted, parted_v = sem("parted"), sem("parted_v")
        attr_cur = sem("attr_cur")
        xj_in = sem("xj_in")
        xi_in = sem("xi_in")
        feat_pool = sem("feat_pool")
        rx1_made = sem("rx1_made")
        feat_dve = sem("feat_dve")
        aux_ready = sem("aux_ready")
        aux_evac = sem("aux_evac")
        rz_made = sem("rz_made")
        msg_done = sem("msg_done")
        hx_done, mx_done, ha_done, ma_done = sem("hx_done"), sem("mx_done"), sem("ha_done"), sem("ma_done")
        rx_done, lx_done, ra_done, la_done = sem("rx_done"), sem("lx_done"), sem("ra_done"), sem("la_done")
        copied = sem("copied")
        made = sem("made")
        xs_ready = sem("xs_ready")
        pool_made = sem("pool_made")
        q_half, q_made = sem("q_half"), sem("q_made")
        a_used = sem("a_used")
        bc_used = sem("bc_used")
        acc_evac = sem("acc_evac")
        rows_in = sem("rows_in")
        srcf_made, same_made, prior_made = sem("srcf_made"), sem("same_made"), sem("prior_made")
        idx_step = sem("idx_step")
        sidx_made = sem("sidx_made")
        scattered = sem("scattered")
        nx_in = [sem(f"nx_in{b}") for b in range(3)]
        na_in = [sem(f"na_in{b}") for b in range(3)]
        n_lin = sem("n_lin")
        n_sum = sem("n_sum")
        n_stats, n_aggr, n_mv, n_sd = sem("n_stats"), sem("n_aggr"), sem("n_mv"), sem("n_sd")
        n_step, n_rs0, n_rs = sem("n_step"), sem("n_rs0"), sem("n_rs")
        n_norm = sem("n_norm")
        n_out = [sem(f"n_out{b}") for b in range(3)]

        NCONST = 7 * 16
        NZERO = N // (P * ZR)
        NSCALE = 13
        srcT_rows = srcT.rearrange("(t j) p -> t j p", j=J)
        block = ctx.enter_context(nc.Block())

        @block.sync
        def _(sp):
            for d, s in ((sel[:, :, :].rearrange("p a b -> p (a b)"), c_sel), (eyeb[:, :], c_eyeb), (eye[:, :], c_eye),
                         (fold[:, :], c_fold), (sum4[:, :], c_sum4), (earlier[:, :], c_earlier), (dump[:, :], c_dump)):
                sp.dma_start(d, s).then_inc(consts_in, 16)
            sp.dma_start(dst_all[:, :], dst).then_inc(tables_in, 16)
            sp.dma_start(src_all[:, :], src).then_inc(tables_in, 16)
            sp.dma_start(attr_all[:, :], attr).then_inc(tables_in, 16)
            sp.wait_ge(small_zeroed, 6)
            sp.dma_start(wa[0:64, 0:64], wm000.rearrange("u a w -> u (a w)")).then_inc(weights_in, 16)
            sp.dma_start(wa[64:128, 0:64], lm0).then_inc(weights_in, 16)
            sp.dma_start(wa[64:128, C:C + F1], wm011.rearrange("u a w -> u (a w)")).then_inc(weights_in, 16)
            for k in range(3):
                col = F0 + F1 * k
                sp.dma_start(wb[32 * k:32 * k + 32, 32 * k:32 * k + 32], lm1).then_inc(weights_in, 16)
                sp.dma_start(wc[32 * k:32 * k + 32, col:col + F1],
                             wm101.rearrange("u a w -> u (a w)")).then_inc(weights_in, 16)
            sp.dma_start(wc[96:128, 0:64], wm110.rearrange("u a w -> u (a w)")).then_inc(weights_in, 16)
            sp.dma_start(wl0[0:64, 0:64], lu0).then_inc(weights_in, 16)
            sp.dma_start(wl0[64:96, 64:96], lu1).then_inc(weights_in, 16)
            sp.dma_start(wl0[96:128, 96:128], lu1).then_inc(weights_in, 16)
            sp.dma_start(wl1[0:32, 128:160], lu1).then_inc(weights_in, 16)
            sp.dma_start(w000[:, :, :], wu000.rearrange("u v w -> (u v) w").rearrange("(c p) w -> p c w", p=128)
                         ).then_inc(weights_in, 16)
            sp.dma_start(w110[:, :, :], wu110.rearrange("u v w -> (u v) w").rearrange("(c p) w -> p c w", p=128)
                         ).then_inc(weights_in, 16)
            sp.dma_start(wt[64:128, 0:GB, :].rearrange("p c (i w) -> p (c i) w", w=F1),
                         wu101.rearrange("u v w -> v u w")).then_inc(weights_in, 16)
            sp.dma_start(wt[0:64, GB:2 * GB, :].rearrange("p c w -> p (c w)"),
                         wu011.rearrange("u v w -> u (v w)")).then_inc(weights_in, 16)
            sp.wait_ge(zeros_made, 1)
            for n in range(NZERO):
                sp.dma_start(acc[n * P * ZR:(n + 1) * P * ZR, :].rearrange("(p r) c -> p (r c)", p=P),
                             zeros[:, :]).then_inc(acc_zeroed, 16)
            sp.dma_start(acc[N:N + DUMP, :], zeros[:, 0:C]).then_inc(acc_zeroed, 16)

            def load_rows(t, first=False):
                if not first:
                    sp.wait_ge(same_made, t)
                sp.dma_start(rows[:, :, :], srcT_rows[t, :, :].rearrange("(a j) p -> a j p", a=1)
                             .to_broadcast((P, J, P))).then_inc(rows_in, 16)

            load_rows(0, first=True)
            with sp.Fori(1, TILES) as t:
                load_rows(t)

            def node_loads(n, b):
                sp.dma_start(xa[:, b, :], xT[0:128, bass.ds(n * T, T)]).then_inc(nx_in[b], 16)
                sp.dma_start(xb[0:32, b, :], xT[128:160, bass.ds(n * T, T)]).then_inc(nx_in[b], 16)
                sp.dma_start(ya[:, b, :], acc[bass.ds(n * T, T), :].rearrange("(p j) c -> p (j c)", p=P)
                             ).then_inc(na_in[b], 16)

            def node_store(n, b):
                sp.wait_ge(n_norm, n + 1)
                sp.dma_start(out[bass.ds(n * T, T), :].rearrange("(p j) c -> p (j c)", p=P), yo[:, b, :]
                             ).then_inc(n_out[b], 16)

            sp.wait_ge(small_zeroed, 7)
            sp.wait_ge(scattered, 16 * J * TILES)
            for n in range(3):
                node_loads(n, n)
            with sp.Fori(1, NT // 3) as i:
                for b in range(3):
                    node_store(3 * i + (b - 3), b)
                    node_loads(3 * i + b, b)
            node_store(NT - 4, 0)
            node_loads(NT - 1, 0)
            for n in range(NT - 3, NT):
                node_store(n, n % 3)
            for b in range(3):
                sp.wait_ge(n_out[b], 16 * ((NT - b + 2) // 3))

        @block.gpsimd
        def _(pool):
            pool.memset(wa[:, :], 0.0).then_inc(small_zeroed, 1)
            pool.memset(wb[:, :], 0.0).then_inc(small_zeroed, 1)
            pool.memset(wc[:, :], 0.0).then_inc(small_zeroed, 1)
            pool.memset(wl0[:, :], 0.0).then_inc(small_zeroed, 1)
            pool.memset(wl1[:, :], 0.0).then_inc(small_zeroed, 1)
            pool.memset(wt[:, :, :], 0.0).then_inc(small_zeroed, 1)
            pool.wait_ge(tables_in, 48)

            def gather(f, first=False):
                if not first:
                    pool.wait_ge(xj_in, 64 * f)
                    pool.wait_ge(xi_in, 64 * f)
                pool.tensor_copy(dcur[:, :], dst_all[:, bass.ds(f * J, J)]).then_inc(idx_cur, 1)
                pool.tensor_copy(scur[:, :], src_all[:, bass.ds(f * J, J)]).then_inc(idx_cur, 1)
                pool.wait_ge(idx_cur, (f + 1) * 2)
                if not first:
                    pool.wait_ge(msg_done, f)
                    pool.wait_ge(rx_done, f)
                pool.sem_inc(parted, 1)
                for j in range(J):
                    pool.indirect_dma_start(G[:, j, F0:F0 + C], None, x,
                                            bass.IndirectOffsetOnAxis(ap=dcur[:, j:j + 1], axis=0)
                                            ).then_inc(xj_in, 16)
                    pool.indirect_dma_start(XI[:, j, :], None, x,
                                            bass.IndirectOffsetOnAxis(ap=scur[:, j:j + 1], axis=0)
                                            ).then_inc(xi_in, 16)

            def features(f):
                pool.wait_ge(xj_in, (f + 1) * 64)
                pool.wait_ge(attr_cur, f + 1)
                e0 = acur[:, :, 3:4]
                pool.tensor_tensor(G[:, :, 0:F0], G[:, :, F0:2 * F0], e0.to_broadcast((P, J, F0)), ALU.mult
                                   ).then_inc(feat_pool, 1)
                pool.tensor_tensor(H[:, :, 0:96], G[:, :, 2 * F0:F0 + C], e0.to_broadcast((P, J, 96)), ALU.mult
                                   ).then_inc(feat_pool, 1)

            def scatter(b, j, pos):
                pool.wait_ge(aux_evac, pos.after(f"ud{j // 2}"))
                pool.wait_ge(sidx_made, b + 1)
                if not (isinstance(b, int) and b == 0 and j == 0):
                    pool.wait_ge(scattered, b * 64 + 16 * j)
                pool.sem_inc(parted, 1)
                pool.indirect_dma_start(acc, bass.IndirectOffsetOnAxis(ap=sidx[:, j:j + 1], axis=0), UD[:, j, :], None,
                                        compute_op=ALU.add).then_inc(scattered, 16)

            def body(t, par, back, front):
                pos = Pos(t, back, front)
                if front:
                    gather(t + 1)
                for g in range(GA):
                    c = 4 * g + 3
                    pool.wait_ge(xs_ready, t * GA + (g + 1))
                    if g < 2:
                        if back:
                            pool.wait_ge(a_used, t * GA + (g - 1))
                    else:
                        pool.wait_ge(a_used, t * GA + (g - 1))
                    pool.tensor_tensor(PA[:, c % 8, :], XS[:, g % 2, :], REP[:, par, 0, :], ALU.mult
                                       ).then_inc(pool_made, 1)
                for c in range(GB):
                    if front and c == 0:
                        features(t + 1)
                    pool.wait_ge(made, t * NV + (v_bc(c, 1, 0) + 1))
                    if c >= 2 or back:
                        pool.wait_ge(bc_used, t * GB + (c - 1))
                    pool.tensor_tensor(QB[:, c % 2, :], PB[:, c % 2, 0, :], PB[:, c % 2, 1, :], ALU.add
                                       ).then_inc(q_half, 1)
                    pool.wait_ge(made, t * NV + (v_bc(c, 2, 0) + 1))
                    pool.wait_ge(q_half, t * GB + (c + 1))
                    pool.tensor_tensor(QB[:, c % 2, :], QB[:, c % 2, :], PB[:, c % 2, 2, :], ALU.add
                                       ).then_inc(q_made, 1)
                    if back and c < J:
                        if isinstance(t, int) and t == 1 and c == 0:
                            pool.wait_ge(acc_zeroed, 16 * (NZERO + 1))
                        scatter(t - 1, c, pos)

            gather(0, first=True)
            features(0)
            body(0, 0, False, True)
            pool.wait_ge(acc_zeroed, 16 * (NZERO + 1))
            with pool.Fori(0, (TILES - 2) // 2) as i:
                body(2 * i + 1, 1, True, True)
                body(2 * i + 2, 0, True, True)
            body(TILES - 1, 1, True, False)
            tail = TailPos()
            for j in range(J):
                scatter(TILES - 1, j, tail)
            pool.wait_ge(bc_used, TILES * GB)
            pool.memset(xb, 0.0).then_inc(small_zeroed, 1)

        @block.scalar
        def _(act):
            copy = ACT.Copy

            act.wait_ge(weights_in, 16 * 18)
            r96 = 96.0 ** -0.5
            for ap, s in ((wa[0:64, 0:64], r96), (wa[64:128, 0:64], 0.125), (wa[64:128, C:C + F1], r96),
                          (wb[:, :], 32.0 ** -0.5), (wc[0:96, :], r96), (wc[96:128, :], (3.0 * 96.0) ** -0.5),
                          (wl0[0:64, :], 0.125), (wl0[64:128, :], 32.0 ** -0.5), (wl1[:, :], 32.0 ** -0.5),
                          (w000[:, :, :], 5120.0 ** -0.5), (w110[:, :, :], (3.0 * 5120.0) ** -0.5),
                          (wt[64:128, 0:GB, :], 1.0 / 64), (wt[0:64, GB:2 * GB, :], 1.0 / 64)):
                act.activation(ap, ap, copy, scale=s).then_inc(weights_ready, 1)

            def evac(dst_ap, pos, name, ps):
                act.wait_ge(aux_ready, pos.after(name))
                act.activation(dst_ap, ps, copy).then_inc(aux_evac, 1)

            def bank(pos, name):
                return aux[pos.bank(name)]

            def part(S, p):
                return S[:, :, :, p, :].rearrange("p j b f -> p (j b) f")

            def flat(a):
                return a[:, :, :].rearrange("p j (b f) -> p (j b) f", f=32)

            def front_piece(name, par, pos):
                ps = bank(pos, name)
                n = int(name[-1])
                if name.startswith("ft"):
                    r = 96 if n == 1 else 128
                    evac(FT[0:r, n, :], pos, name, ps[0:r, 0:T])
                elif name.startswith("m"):
                    evac(M[:, 2 * n:2 * n + 2, :], pos, name,
                         ps[0:P, 0:2 * (C + F1)].rearrange("p (j c) -> p j c", j=2))
                elif name.startswith("sx"):
                    evac(ST[:, par, n, :], pos, name, ps[0:96, 0:T])
                elif name.startswith("sa"):
                    evac(ST[:, par, 5 + n, :], pos, name, ps[0:96, 0:T])
                else:
                    evac(REP[:, par, n, :], pos, name, ps[:, 0:T])

            def split_x(f, step):
                if step == 0:
                    act.wait_ge(xi_in, (f + 1) * 64)
                    act.activation(part(SX, 0), flat(XI), copy).then_inc(hx_done, 1)
                else:
                    act.wait_ge(rx_done, f + 1)
                    act.activation(part(SX, 1), flat(RX), copy).then_inc(mx_done, 1)

            def split_a(f, step):
                if step == 0:
                    act.wait_ge(msg_done, f + 1)
                    act.activation(SA[:, :, :, 0, :], M[:, :, 0:C].rearrange("p j (b f) -> p j b f", f=32), copy
                                   ).then_inc(ha_done, 1)
                else:
                    act.wait_ge(ra_done, f + 1)
                    act.activation(part(SA, 1), flat(RA), copy).then_inc(ma_done, 1)

            def acc_out(b):
                act.wait_ge(bc_used, (b + 1) * GB)
                act.activation(U0[:, :], acc0[:, 0:T], copy).then_inc(acc_evac, 1)
                act.activation(U1[:, :], acc1[0:96, 0:T], copy).then_inc(acc_evac, 1)

            def back_piece(name, b, pos, first=False):
                n = int(name[-1])
                if name == "ud0" and not first:
                    act.wait_ge(scattered, b * 64)
                evac((UL if name[1] == "l" else UD)[:, 2 * n:2 * n + 2, :], pos, name,
                     bank(pos, name)[0:P, 0:2 * C].rearrange("p (j c) -> p j c", j=2))

            def body(t, par, back, front):
                pos = Pos(t, back, front)
                for g in range(GA):
                    act.wait_ge(copied, t * NX + (4 * g + 4))
                    if g >= 2 or back:
                        act.wait_ge(pool_made, t * GA + (g - 1))
                    act.activation(XS[:, g % 2, :], copies[3][:, 0:T], copy).then_inc(xs_ready, 1)
                    if back:
                        if g == 0:
                            acc_out(t - 1)
                        for name in BACK_AT.get(g, []):
                            back_piece(name, t - 1, pos, isinstance(t, int) and t == 1)
                for c in range(GB):
                    if c >= 2:
                        act.wait_ge(made, t * NV + (v_bc(c - 2, 2, 2) + 1))
                    evac(TS[:, (2 * c) % 4, :], pos, f"t101_{c}", bank(pos, f"t101_{c}")[:, 0:T])
                    evac(TS[:, (2 * c) % 4 + 1, :], pos, f"t011_{c}", bank(pos, f"t011_{c}")[:, 0:T])
                    if front:
                        f = t + 1
                        if c == 3:
                            split_a(f, 0)
                        if c == 4:
                            split_a(f, 1)
                        for name in FRONT_AT.get(GA + c, []):
                            front_piece(name, 1 - par, pos)
                        if c < 2:
                            split_x(f, c)

            pro = ProloguePos()
            split_x(0, 0)
            split_x(0, 1)
            for name in FRONT:
                if name == "sa0":
                    split_a(0, 0)
                    split_a(0, 1)
                front_piece(name, 0, pro)
            body(0, 0, False, True)
            with act.Fori(0, (TILES - 2) // 2) as i:
                body(2 * i + 1, 1, True, True)
                body(2 * i + 2, 0, True, True)
            body(TILES - 1, 1, True, False)
            tail = TailPos()
            acc_out(TILES - 1)
            for name in ("ul0", "ul1", "ud0", "ud1"):
                back_piece(name, TILES - 1, tail)

            def node_sd(n, b):
                act.wait_ge(n_mv, n + 1)
                act.activation(sd[:, b, :], ve[:, b, :], ACT.Sqrt).then_inc(n_sd, 1)

            def node_norm(n, b, left):
                act.wait_ge(n_rs, n + 1)
                if left is not None:
                    act.wait_ge(n_out[b], left)
                for j in range(J):
                    last = act.activation(yo[:, b, j * C:(j + 1) * C], ya[:, b, j * C:(j + 1) * C], ACT.Identity,
                                          bias=nb[:, b, j:j + 1], scale=rs[:, b, j:j + 1])
                last.then_inc(n_norm, 1)

            for n in range(6):
                node_sd(n, n % 3)
                if n:
                    node_norm(n - 1, (n - 1) % 3, 16 if n > 3 else None)
            with act.Fori(2, NT // 3) as i:
                for b in range(3):
                    node_sd(3 * i + b, b)
                    node_norm(3 * i + (b - 1), (b - 1) % 3, (i - 1) * 16 if b == 0 else i * 16)
            n = NT - 1
            node_sd(n, n % 3)
            node_norm(n - 1, (n - 1) % 3, ((n - 1) // 3) * 16)
            node_norm(n, n % 3, (n // 3) * 16)

        @block.vector
        def _(dve):
            def part(S, p):
                return S[:, :, :, p, :].rearrange("p j b f -> p (j b) f")

            def flat(a):
                return a[:, :, :].rearrange("p j (b f) -> p (j b) f", f=32)

            def load_attr(f, first=False):
                if not first:
                    dve.wait_ge(feat_pool, f * 2)
                dve.tensor_copy(acur[:, :, :].rearrange("p j a -> p (j a)"), attr_all[:, bass.ds(f * (4 * J), 4 * J)]
                                ).then_inc(attr_cur, 1)

            def dot_r(f):
                dve.wait_ge(xj_in, (f + 1) * 64)
                dve.wait_ge(attr_cur, f + 1)
                r = acur[:, :, 0:3].rearrange("p j (k a) -> p j k a", a=1).to_broadcast((P, J, 3, F1))
                dve.tensor_tensor(rx1[:, :, :, :], G[:, :, 2 * F0:F0 + C].rearrange("p j (k u) -> p j k u", k=3), r,
                                  ALU.mult).then_inc(rx1_made, 1)
                dve.wait_ge(rx1_made, f + 1)
                dve.tensor_reduce(H[:, :, 96:128], rx1[:, :, :, :].rearrange("p j k u -> p j u k"), AX.X, ALU.add
                                  ).then_inc(feat_dve, 1)

            def message(f, pos):
                dve.wait_ge(aux_evac, pos.after("m1"))
                z = M[:, :, C:C + F1].rearrange("p j (a w) -> p j a w", a=1).to_broadcast((P, J, 3, F1))
                r = acur[:, :, 0:3].rearrange("p j (k a) -> p j k a", a=1).to_broadcast((P, J, 3, F1))
                dve.tensor_tensor(rz[:, :, :, :], z, r, ALU.mult).then_inc(rz_made, 1)
                dve.wait_ge(rz_made, f + 1)
                a1 = M[:, :, F0:C]
                dve.tensor_tensor(a1, a1, rz[:, :, :, :].rearrange("p j k w -> p j (k w)"), ALU.add
                                  ).then_inc(msg_done, 1)

            def rest_x(f, step):
                if step == 0:
                    dve.wait_ge(hx_done, f + 1)
                    dve.tensor_tensor(flat(RX), flat(XI), part(SX, 0), ALU.subtract).then_inc(rx_done, 1)
                else:
                    dve.wait_ge(mx_done, f + 1)
                    dve.tensor_tensor(part(SX, 2), flat(RX), part(SX, 1), ALU.subtract).then_inc(lx_done, 1)

            def rest_a(f, step):
                if step == 0:
                    dve.wait_ge(ha_done, f + 1)
                    dve.tensor_tensor(RA[:, :, :].rearrange("p j (b f) -> p j b f", f=32),
                                      M[:, :, 0:C].rearrange("p j (b f) -> p j b f", f=32), SA[:, :, :, 0, :],
                                      ALU.subtract).then_inc(ra_done, 1)
                else:
                    dve.wait_ge(ma_done, f + 1)
                    dve.tensor_tensor(part(SA, 2), flat(RA), part(SA, 1), ALU.subtract).then_inc(la_done, 1)

            def repeats(b, step, first=False):
                if step == 0:
                    dve.tensor_copy(srcf[:, :], src_all[:, bass.ds(b * J, J)]).then_inc(srcf_made, 1)
                    dve.wait_ge(srcf_made, b + 1)
                    dve.wait_ge(rows_in, (b + 1) * 16)
                    dve.tensor_tensor(same[:, :, :], rows[:, :, :],
                                      srcf[:, :].rearrange("p (j a) -> p j a", a=1).to_broadcast((P, J, P)),
                                      ALU.is_equal).then_inc(same_made, 1)
                elif step == 1:
                    dve.wait_ge(same_made, b + 1)
                    dve.tensor_tensor(prior[:, :, :], same[:, :, :],
                                      earlier[:, :].rearrange("p (a e) -> p a e", a=1).to_broadcast((P, J, P)),
                                      ALU.mult).then_inc(prior_made, 1)
                    dve.wait_ge(prior_made, b + 1)
                    dve.tensor_reduce(dup[:, :], prior[:, :, :], AX.X, ALU.add).then_inc(idx_step, 1)
                else:
                    dve.tensor_scalar(todump[:, :], srcf[:, :], -1.0, dump[:, 0:1], ALU.mult, ALU.add
                                      ).then_inc(idx_step, 1)
                    dve.wait_ge(idx_step, b * 4 + 2)
                    dve.tensor_scalar(dup[:, :], dup[:, :], 1.0, None, ALU.min).then_inc(idx_step, 1)
                    dve.wait_ge(idx_step, b * 4 + 3)
                    dve.tensor_tensor(todump[:, :], todump[:, :], dup[:, :], ALU.mult).then_inc(idx_step, 1)
                    dve.wait_ge(idx_step, b * 4 + 4)
                    if not first:
                        dve.wait_ge(scattered, b * 64)
                    dve.tensor_tensor(sidx[:, :], todump[:, :], srcf[:, :], ALU.add).then_inc(sidx_made, 1)

            def body(t, par, back, front):
                pos = Pos(t, back, front)
                dve.wait_ge(aux_evac, pos.base + pos.start)
                for g in range(GA):
                    if g >= 2 or back:
                        dve.wait_ge(a_used, t * GA + (g - 1))
                    for i in range(3):
                        c = 4 * g + i
                        dve.wait_ge(copied, t * NX + (c + 1))
                        dve.tensor_tensor(PA[:, c % 8, :], copies[i][:, 0:T], REP[:, par, 0, :], ALU.mult
                                          ).then_inc(made, 1)
                    if back and g < 3:
                        repeats(t - 1, g, isinstance(t, int) and t == 1)
                for c in range(GB):
                    if front:
                        f = t + 1
                        if c == 0:
                            load_attr(f)
                            dot_r(f)
                        if c in (1, 2):
                            rest_x(f, c - 1)
                        if c == 3:
                            message(f, pos)
                        if c in (4, 5):
                            rest_a(f, c - 4)
                    if c >= 2 or back:
                        dve.wait_ge(q_made, t * GB + (c - 1))
                        dve.wait_ge(bc_used, t * GB + (c - 1))
                    dve.wait_ge(aux_evac, pos.after(f"t011_{c}"))
                    for k in range(3):
                        n = 4 * GA + 6 * c + 2 * k
                        dve.wait_ge(copied, t * NX + (n + 1))
                        dve.tensor_tensor(PB[:, c % 2, k, :], copies[n % 4][:, 0:T], REP[:, par, 1 + k, :], ALU.mult
                                          ).then_inc(made, 1)
                        dve.tensor_tensor(ZB[:, c % 2, k, :], copies[n % 4][:, 0:T], TS[:, (2 * c) % 4, :], ALU.mult
                                          ).then_inc(made, 1)
                        dve.wait_ge(copied, t * NX + (n + 2))
                        dve.tensor_tensor(ZC[:, c % 2, k, :], copies[(n + 1) % 4][:, 0:T], TS[:, (2 * c) % 4 + 1, :],
                                          ALU.mult).then_inc(made, 1)

            dve.memset(zeros[:, :], 0.0).then_inc(zeros_made, 1)
            dve.wait_ge(weights_ready, NSCALE)
            dve.wait_ge(consts_in, NCONST)
            dve.scalar_tensor_tensor(wl0[:, 0:128], eye[:, :], 2.0, wl0[:, 0:128], ALU.mult, ALU.add
                                     ).then_inc(wl_ready, 1)
            dve.scalar_tensor_tensor(wl1[0:32, 128:160], eye[0:32, 0:32], 2.0, wl1[0:32, 128:160], ALU.mult, ALU.add
                                     ).then_inc(wl_ready, 1)
            dve.wait_ge(tables_in, 48)
            pro = ProloguePos()
            load_attr(0, first=True)
            dot_r(0)
            rest_x(0, 0)
            rest_x(0, 1)
            message(0, pro)
            rest_a(0, 0)
            rest_a(0, 1)
            body(0, 0, False, True)
            with dve.Fori(0, (TILES - 2) // 2) as i:
                body(2 * i + 1, 1, True, True)
                body(2 * i + 2, 0, True, True)
            body(TILES - 1, 1, True, False)
            for step in range(3):
                repeats(TILES - 1, step)

            def node_stats(n, b, group):
                dve.wait_ge(n_lin, n + 1)
                dve.wait_ge(na_in[b], (group + 1) * 16)
                for h in range(2):
                    y = ya[:, b, 2 * C * h:2 * C * (h + 1)]
                    dve.tensor_tensor(y, pairs[b][h][0:P, 0:2 * C], y, ALU.add).then_inc(n_sum, 1)
                dve.wait_ge(n_sum, (n + 1) * 2)
                for j in range(J):
                    last = dve.bn_stats(stats[:, b, j, :], ya[:, b, j * C:(j + 1) * C])
                last.then_inc(n_stats, 1)
                dve.wait_ge(n_stats, n + 1)
                dve.sem_inc(parted_v, 1)
                for j in range(J):
                    last = dve.bn_aggr(mv[:, b, j, :], stats[:, b, j, :])
                last.then_inc(n_aggr, 1)
                dve.wait_ge(n_aggr, n + 1)
                dve.tensor_scalar(ve[:, b, :], mv[:, b, :, 1], EPS, None, ALU.add).then_inc(n_mv, 1)

            def node_scale(n, b):
                dve.wait_ge(n_sd, n + 1)
                dve.reciprocal(r0[:, b, :], sd[:, b, :]).then_inc(n_step, 1)
                dve.wait_ge(n_step, n * 4 + 1)
                dve.tensor_tensor(hv[:, b, :], r0[:, b, :], r0[:, b, :], ALU.mult).then_inc(n_step, 1)
                dve.wait_ge(n_step, n * 4 + 2)
                dve.tensor_tensor(hv[:, b, :], hv[:, b, :], ve[:, b, :], ALU.mult).then_inc(n_step, 1)
                dve.wait_ge(n_step, n * 4 + 3)
                dve.tensor_scalar(hv[:, b, :], hv[:, b, :], -0.5, 1.5, ALU.mult, ALU.add).then_inc(n_step, 1)
                dve.wait_ge(n_step, n * 4 + 4)
                dve.tensor_tensor(rs[:, b, :], r0[:, b, :], hv[:, b, :], ALU.mult).then_inc(n_rs0, 1)
                dve.wait_ge(n_rs0, n + 1)
                dve.scalar_tensor_tensor(nb[:, b, :], mv[:, b, :, 0], -1.0, rs[:, b, :], ALU.mult, ALU.mult
                                         ).then_inc(n_rs, 1)

            for n in range(3):
                node_stats(n, n, 0)
                if n:
                    node_scale(n - 1, n - 1)
            with dve.Fori(1, NT // 3) as i:
                for b in range(3):
                    node_stats(3 * i + b, b, i)
                    node_scale(3 * i + (b - 1), (b - 1) % 3)
            n = NT - 1
            node_stats(n, n % 3, n // 3)
            node_scale(n - 1, (n - 1) % 3)
            node_scale(n, n % 3)

        @block.tensor
        def _(pe):
            def aux_bank(pos, name):
                after = pos.after(name)
                if not (isinstance(after, int) and after <= 2):
                    pe.wait_ge(aux_evac, after - 2)
                return aux[pos.bank(name)]

            def front_piece(name, f, par, pos):
                n = int(name[-1])
                if name == "ft0":
                    pe.wait_ge(feat_pool, f * 2 + 2)
                    pe.wait_ge(feat_dve, f + 1)
                elif name == "m0":
                    pe.wait_ge(aux_evac, pos.after("ft2"))
                elif name == "sx0":
                    pe.wait_ge(lx_done, f + 1)
                elif name == "sa0":
                    pe.wait_ge(la_done, f + 1)
                elif name == "rep0":
                    pe.wait_ge(aux_evac, pos.after("sa4"))
                ps = aux_bank(pos, name)
                if name.startswith("ft"):
                    for j in range(J):
                        f_in = (G[:, j, 0:128], G[:, j, 128:224], H[:, j, :])[n]
                        m = 96 if n == 1 else 128
                        last = pe.matmul(ps[0:m, j * P:(j + 1) * P], f_in, eye[0:P, 0:P], start=True, stop=True)
                elif name.startswith("m"):
                    for jj in range(2):
                        e = slice((2 * n + jj) * P, (2 * n + jj + 1) * P)
                        o = jj * (C + F1)
                        pe.matmul(ps[0:P, o:o + C + F1], FT[:, 0, e], wa[:, :], start=True, stop=False)
                        pe.matmul(ps[0:P, o + F0:o + C], FT[0:96, 1, e], wb[:, :], start=False, stop=False)
                        last = pe.matmul(ps[0:P, o:o + C], FT[:, 2, e], wc[:, :], start=False, stop=True)
                elif name.startswith("s"):
                    S = SX if name[1] == "x" else SA
                    for j in range(J):
                        last = pe.matmul(ps[0:96, j * P:(j + 1) * P], S[:, j, n, :, :].rearrange("p a f -> p (a f)"),
                                         eyeb[0:P, 0:P], start=True, stop=True)
                elif n == 0:
                    for b in range(2):
                        last = pe.matmul(ps[:, 0:T], sel[:, REPA + b, :], ST[:, par, 5 + b, :],
                                         start=(b == 0), stop=(b == 1))
                elif n < 4:
                    last = pe.matmul(ps[:, 0:T], sel[:, REP4, :], ST[:, par, 6 + n, :], start=True, stop=True)
                else:
                    for q, b in enumerate((0, 1, 5, 6)):
                        last = pe.matmul(ps[:, 0:T], sel[:, STK + q, :], ST[:, par, b, :],
                                         start=(q == 0), stop=(q == 3))
                last.then_inc(aux_ready, 1)

            def back_piece(name, b, pos):
                n = int(name[-1])
                if name == "ul0":
                    pe.wait_ge(acc_evac, b * 2 + 2)
                elif name == "ud0":
                    pe.wait_ge(same_made, b + 1)
                    pe.wait_ge(aux_evac, pos.after("ul1"))
                ps = aux_bank(pos, name)
                for jj in range(2):
                    j, o = 2 * n + jj, jj * C
                    if name[1] == "l":
                        pe.matmul(ps[0:P, o:o + F0], U0[:, j * P:(j + 1) * P], fold[:, :], start=True, stop=True)
                        last = pe.matmul(ps[0:P, o + F0:o + C], U1[:, j * P:(j + 1) * P], eye[0:96, 0:96],
                                         start=True, stop=True)
                    else:
                        last = pe.matmul(ps[0:P, o:o + C], same[:, j, :], UL[:, j, :], start=True, stop=True)
                last.then_inc(aux_ready, 1)

            def copy_features(t, n, back, lhsT, rhs):
                if n >= 4:
                    kind, count = occupant_done(n - 4)
                    pe.wait_ge(made if kind == "v" else xs_ready, t * (NV if kind == "v" else GA) + count)
                elif back:
                    kind, count = occupant_done(NX - 4 + n)
                    pe.wait_ge(made, t * NV + (count - NV))
                pe.matmul(copies[n % 4][:, 0:T], lhsT, rhs, start=True, stop=True).then_inc(copied, 1)

            def contract_a(t, g):
                for i in range(4):
                    c = 4 * g + i
                    if i < 3:
                        pe.wait_ge(made, t * NV + (v_a(g, i) + 1))
                    else:
                        pe.wait_ge(pool_made, t * GA + (g + 1))
                    h = 64 * (c % 2)
                    last = pe.matmul(acc0[h:h + 64, 0:T], w000[:, c, :], PA[:, c % 8, :], start=(c < 2), stop=False)
                last.then_inc(a_used, 1)

            def contract_bc(t, c):
                h = 64 * (c % 2)
                pe.wait_ge(q_made, t * GB + (c + 1))
                pe.matmul(acc0[h:h + 64, 0:T], w110[:, c, :], QB[:, c % 2, :], start=False, stop=(c >= GB - 2))
                for a, Z in ((0, ZB), (1, ZC)):
                    for k in range(3):
                        pe.wait_ge(made, t * NV + (v_bc(c, k, 1 + a) + 1))
                        last = pe.matmul(acc1[32 * k:32 * k + 32, 0:T], sum4[:, :], Z[:, c % 2, k, :],
                                         start=(c == 0 and a == 0), stop=(c == GB - 1 and a == 1))
                last.then_inc(bc_used, 1)

            def body(t, par, back, front):
                pos = Pos(t, back, front)
                pe.wait_ge(aux_evac, pos.base + pos.start)
                for g in range(GA):
                    for i in range(4):
                        c = 4 * g + i
                        copy_features(t, c, back, sel[:, SEL2 + c % 16, :], ST[:, par, c // 16, :])
                    if g == 0:
                        if back:
                            contract_bc(t - 1, GB - 1)
                    else:
                        if g == 1 and back:
                            pe.wait_ge(acc_evac, t * 2)
                        contract_a(t, g - 1)
                    if back:
                        for name in BACK_AT.get(g, []):
                            back_piece(name, t - 1, pos)
                for c in range(GB):
                    for w, name in ((c, f"t101_{c}"), (GB + c, f"t011_{c}")):
                        ps = aux_bank(pos, name)
                        pe.matmul(ps[:, 0:T], wt[:, w, :], REP[:, par, 4, :], start=True, stop=True
                                  ).then_inc(aux_ready, 1)
                    for k in range(3):
                        n = 4 * GA + 6 * c + 2 * k
                        copy_features(t, n, back, sel[:, SEL4 + c, :], ST[:, par, 2 + k, :])
                        copy_features(t, n + 1, back, sel[:, SEL4 + c, :], ST[:, par, 7 + k, :])
                    if c == 0:
                        contract_a(t, GA - 1)
                    else:
                        contract_bc(t, c - 1)
                    if front:
                        for name in FRONT_AT.get(GA + c, []):
                            front_piece(name, t + 1, 1 - par, pos)

            pe.wait_ge(consts_in, NCONST)
            pe.wait_ge(weights_ready, NSCALE)
            pro = ProloguePos()
            for name in FRONT:
                front_piece(name, 0, 0, pro)
            body(0, 0, False, True)
            with pe.Fori(0, (TILES - 2) // 2) as i:
                body(2 * i + 1, 1, True, True)
                body(2 * i + 2, 0, True, True)
            body(TILES - 1, 1, True, False)
            contract_bc(TILES - 1, GB - 1)
            tail = TailPos()
            for name in ("ul0", "ul1", "ud0", "ud1"):
                back_piece(name, TILES - 1, tail)

            pe.wait_ge(wl_ready, 2)

            def node_lin(n, b, group, reuse):
                if reuse:
                    pe.wait_ge(n_sum, 2 * n - 4)
                pe.wait_ge(nx_in[b], (group + 1) * 32)
                for j in range(J):
                    ps = pairs[b][j // 2][0:P, (j % 2) * C:(j % 2 + 1) * C]
                    pe.matmul(ps, xa[:, b, j * P:(j + 1) * P], wl0[:, :], start=True, stop=False)
                    last = pe.matmul(ps, xb[:, b, j * P:(j + 1) * P], wl1[:, :], start=False, stop=True)
                last.then_inc(n_lin, 1)

            for n in range(3):
                node_lin(n, n, 0, False)
            with pe.Fori(1, NT // 3) as i:
                for b in range(3):
                    node_lin(3 * i + b, b, i, True)
            node_lin(NT - 1, (NT - 1) % 3, (NT - 1) // 3, True)


_INS = ["x", "xT", "src", "srcT", "dst", "attr", "wm000", "wm011", "wm101", "wm110", "lm0", "lm1",
        "wu000", "wu011", "wu101", "wu110", "lu0", "lu1", "c_sel", "c_eyeb", "c_eye", "c_fold", "c_sum4",
        "c_earlier", "c_dump"]


def kernel(x, src, dst, edge_attr_4, node_vec1, **w):
    import ml_dtypes
    import concourse.bacc as _bacc
    from concourse.bass_utils import run_bass_kernel_spmd as _run

    x = np.asarray(x)
    xk = np.concatenate([x[:, :F0], x[:, F0:].reshape(N, F1, 3).transpose(0, 2, 1).reshape(N, 3 * F1)], 1)
    xT = xk.reshape(NT, P, J, C).transpose(3, 0, 2, 1).reshape(C, N)
    arrays = {
        "x": xk, "xT": xT,
        "src": np.asarray(src).reshape(P, COLS), "srcT": np.asarray(src).reshape(P, COLS).T,
        "dst": np.asarray(dst).reshape(P, COLS), "attr": np.asarray(edge_attr_4).reshape(P, COLS * 4),
    }
    for name in _INS[6:18]:
        key = "L0_gnn_" + name
        arrays[name] = np.asarray(w[key])
    for name, (a, dt) in constants().items():
        arrays[name] = np.asarray(a, dtype=ml_dtypes.bfloat16 if dt == "bfloat16" else dt)
    arrays = {k + "_dram": np.ascontiguousarray(v) for k, v in arrays.items()}

    nc = _bacc.Bacc("TRN2", target_bir_lowering=False, num_devices=1)
    args = [nc.dram_tensor(n + "_dram", arrays[n + "_dram"].shape, mybir.dt.from_np(arrays[n + "_dram"].dtype),
                           kind="ExternalInput").ap() for n in _INS]
    out = nc.dram_tensor("out_dram", (N, C), mybir.dt.float32, kind="ExternalOutput").ap()
    build(nc, *args, out)
    got = _run(nc, [arrays], core_ids=[0]).results[0]["out_dram"]
    return np.concatenate([got[:, :F0], got[:, F0:].reshape(N, 3, F1).transpose(0, 2, 1).reshape(N, 3 * F1)], 1)
```

```python
import concourse.bass as bass
from concourse import mybir
from contextlib import ExitStack
import numpy as np

N, E, F0, F1, C = 50000, 25000, 64, 32, 160
P = 125
J = 4
T = P * J
TILES = E // T
COLS = E // P
NT = N // T
NA = F0 // 2
GA = NA // 4
GB = F1 // 4
DUMP = P
ZR = 10
EPS = 1e-5

SEL2, SEL4, REP4, REPA, STK = 0, 16, 24, 25, 27
NSEL = 31


def selectors():
    k = np.arange(96)[:, None] % 32
    m = np.arange(128)[None, :]
    parts = [k == 2 * c + m // 64 for c in range(16)]
    parts += [k == 4 * c + m // 32 for c in range(8)]
    parts += [k == m % 32]
    parts += [k + 32 * b == m % 64 for b in range(2)]
    parts += [(k == m % 32) & (m // 32 == q) for q in range(4)]
    return np.concatenate([np.broadcast_to(a, (96, 128)) for a in parts], 1)


def constants():
    p = np.arange(128)
    vec = np.arange(96)
    perm = np.eye(96)
    return {
        "c_sel": (selectors(), "bfloat16"),
        "c_eyeb": (np.eye(128), "bfloat16"),
        "c_eye": (np.eye(128), "float32"),
        "c_fold": (p[:, None] % 64 == np.arange(64)[None, :], "float32"),
        "c_sum4": (p[:, None] % 32 == np.arange(32)[None, :], "float32"),
        "c_earlier": (np.arange(P)[None, :] < np.arange(P)[:, None], "float32"),
        "c_dump": (N + np.arange(P)[:, None], "float32"),
    }


SLOTS = GA
BACK_AT = {(4, 0): ["ul0"], (5, 0): ["ul1"], (5, 4): ["ud0"], (6, 2): ["ud1"]}
FRONT_AT = {(0, 4): ["ft0"], (1, 1): ["ft1"], (1, 4): ["ft2"], (2, 2): ["m0"], (3, 2): ["m1"],
            (3, 0): ["sx0"], (3, 4): ["sx1"], (4, 1): ["sx2"], (4, 2): ["sx3"], (4, 4): ["sx4"],
            (6, 0): ["sa0"], (6, 1): ["sa1"], (6, 3): ["sa2", "sa3"], (6, 4): ["sa4"],
            (7, 0): ["rep4"], (7, 1): ["rep0"], (7, 2): ["rep1"], (7, 3): ["rep2"], (7, 4): ["rep3"]}
T_AT = {(s, 0): [f"t101_{s}"] for s in range(SLOTS)}
T_AT |= {(s - 1, 4): [f"t011_{s}"] for s in range(1, SLOTS)}
T_AT[(0, 2)] = ["t011_0"]
FRONT = [a for at in sorted(FRONT_AT) for a in FRONT_AT[at]]
BACK = [a for at in sorted(BACK_AT) for a in BACK_AT[at]]
NBACK = len(BACK)


def aux_order(back, front):
    order = []
    for s in range(SLOTS):
        for point in range(5):
            order += T_AT.get((s, point), [])
            if back:
                order += BACK_AT.get((s, point), [])
            if front:
                order += FRONT_AT.get((s, point), [])
    return order


NAUX = len(aux_order(True, True))
assert NAUX % 2 == 0 and NBACK % 2 == 0 and len(FRONT) % 2 == 0


class Pos:

    def __init__(self, before, offset, order):
        self.before, self.offset = before, offset
        self.at = {a: n for n, a in enumerate(order)}

    def bank(self, name):
        return (self.offset + self.at[name]) % 2

    def after(self, name):
        return self.before + (self.offset + self.at[name] + 1)

    def start(self):
        return self.before + self.offset


def prologue_pos():
    return Pos(0, 0, FRONT)


def body_pos(t, back, front):
    return Pos(t * NAUX, len(FRONT) - (NBACK if back else 0), aux_order(back, front))


def tail_pos():
    return Pos((TILES - 1) * NAUX, len(FRONT) - NBACK + len(aux_order(True, False)), BACK)


COPIES = ["A01", "X01", "V01", "A23", "XV2"]
NX = SLOTS * len(COPIES)
PRODUCTS = ["A01", "P01", "B01", "C01", "A23", "P2", "B2", "C2"]
NV = SLOTS * len(PRODUCTS)
FREES = {"A01": "A01", "X01": "B01", "V01": "C01", "A23": "A23", "XV2": "C2"}
GATHER_SLOT = 2
ADDS = [(0, 1, 2) if s < SLOTS - J else (0, 1) for s in range(SLOTS)]
NZ = sum(len(a) for a in ADDS)


def copy_use(s, name):
    return len(COPIES) * s + COPIES.index(name)


def v_after(s, name):
    return len(PRODUCTS) * s + PRODUCTS.index(name) + 1


def z_after(s, k=None):
    return sum(len(a) for a in ADDS[:s]) + (len(ADDS[s]) if k is None else k + 1)


def build(nc, x, xT, src, srcT, dst, attr, wm000, wm011, wm101, wm110, lm0, lm1, wu000, wu011, wu101, wu110,
          lu0, lu1, c_sel, c_eyeb, c_eye, c_fold, c_sum4, c_earlier, c_dump, out):
    f32, b16, i32 = mybir.dt.float32, mybir.dt.bfloat16, mybir.dt.int32
    ALU, ACT, AX = mybir.AluOpType, mybir.ActivationFunctionType, mybir.AxisListType
    ctx = ExitStack()
    with ctx:
        def sb(name, shape, dt=f32):
            return ctx.enter_context(nc.sbuf_tensor(name, shape, dt))

        def sem(name):
            return ctx.enter_context(nc.semaphore(name))

        acc = nc.dram_tensor("acc", (N + DUMP, C), f32, kind="Internal").ap()

        sel = sb("sel", [96, NSEL, 128], b16)
        eyeb = sb("eyeb", [128, 128], b16)
        eye = sb("eye", [128, 128])
        fold = sb("fold", [128, 64])
        sum4 = sb("sum4", [128, 32])
        earlier = sb("earlier", [P, P])
        dump = sb("dump", [P, 1])
        zeros = sb("zeros", [P, 1, 2 * C])
        w000 = sb("w000", [128, NA, F0])
        w110 = sb("w110", [128, GB, F0])
        wt = sb("wt", [128, 2 * GB, 128])
        wa = sb("wa", [128, C + F1])
        wb = sb("wb", [96, 96])
        wc = sb("wc", [128, C])
        wl0 = sb("wl0", [128, C])
        wl1 = sb("wl1", [128, C])
        src_all = sb("src_all", [P, COLS + J], i32)
        dst_all = sb("dst_all", [P, COLS + J], i32)
        attr_all = sb("attr_all", [P, COLS * 4])
        dcur = sb("dcur", [P, J], i32)
        scur = sb("scur", [P, J], i32)
        acur = sb("acur", [P, J, 4])
        G = sb("G", [P, J, F0 + C])
        H = sb("H", [P, J, 128])
        rx1 = sb("rx1", [P, J, 3, F1])
        XI = sb("XI", [P, J, C])
        M = sb("M", [P, J, C + F1])
        rz = sb("rz", [P, J, 3, F1])
        R = sb("R", [P, J, C])
        SX = sb("SX", [P, J, 5, 3, 32], b16)
        SA = sb("SA", [P, J, 5, 3, 32], b16)
        FT = sb("FT", [128, 3, T])
        ST = sb("ST", [96, 2, 10, T], b16)
        REP = sb("REP", [128, 2, 5, T])
        arena = sb("arena", [128, 42, T])
        PA = arena[:, 0:8, :]
        PB = arena[:, 8:14, :].rearrange("p (g k) e -> p g k e", g=2)
        ZB = arena[:, 14:26, :].rearrange("p (g k) e -> p g k e", g=4)
        ZC = arena[:, 26:38, :].rearrange("p (g k) e -> p g k e", g=4)
        TS = arena[:, 38:42, :]
        QB = sb("QB", [128, 2, T])
        U0 = sb("U0", [128, T])
        U1 = sb("U1", [96, T])
        UL = sb("UL", [P, J, C])
        UD = sb("UD", [P, J, C])
        rows = sb("rows", [P, J, P], i32)
        srcf = sb("srcf", [P, J])
        same = sb("same", [P, J, P])
        prior = sb("prior", [P, J, P])
        dup = sb("dup", [P, J])
        todump = sb("todump", [P, J])
        sidx = sb("sidx", [P, J], i32)
        xa = arena[:, 0:3, :]
        xb = arena[:, 3:6, :]
        ya = arena[0:P, 6:14, :].rearrange("p n e -> p (n e)")[:, 0:3 * J * C].rearrange("p (b f) -> p b f", b=3)
        yo = arena[0:P, 14:22, :].rearrange("p n e -> p (n e)")[:, 0:3 * J * C].rearrange("p (b f) -> p b f", b=3)
        stats = sb("stats", [P, 3, J, 6])
        mv = sb("mv", [P, 3, J, 2])
        ve, sd, r0, hv, rs, nb = (sb(n, [P, 3, J]) for n in ("ve", "sd", "r0", "hv", "rs", "nb"))

        copies = ctx.enter_context(nc.psum_tensor("copies", [128, 4, 512], f32))
        acc0 = ctx.enter_context(nc.psum_tensor("acc0", [128, 512], f32))
        acc1 = ctx.enter_context(nc.psum_tensor("acc1", [128, 512], f32))
        pairs = [[copies[:, 0, :], copies[:, 1, :]], [copies[:, 2, :], copies[:, 3, :]], [acc0[:, :], acc1[:, :]]]
        aux = [ctx.enter_context(nc.psum_tensor(f"aux{b}", [128, 512], f32)) for b in range(2)]

        consts_in = sem("consts_in")
        weights_in = sem("weights_in")
        tables_in = sem("tables_in")
        small_zeroed = sem("small_zeroed")
        zeros_made = sem("zeros_made")
        acc_zeroed = sem("acc_zeroed")
        weights_ready = sem("weights_ready")
        wl_ready = sem("wl_ready")
        idx_cur = sem("idx_cur")
        parted, parted_v = sem("parted"), sem("parted_v")
        attr_cur = sem("attr_cur")
        xj_in = sem("xj_in")
        xi_in = sem("xi_in")
        feat_pool = sem("feat_pool")
        rx1_made = sem("rx1_made")
        feat_dve = sem("feat_dve")
        aux_ready = sem("aux_ready")
        aux_evac = sem("aux_evac")
        rz_made = sem("rz_made")
        msg_done = sem("msg_done")
        hx_done, mx_done, ha_done, ma_done = sem("hx_done"), sem("mx_done"), sem("ha_done"), sem("ma_done")
        rx_done, lx_done, ra_done, la_done = sem("rx_done"), sem("lx_done"), sem("ra_done"), sem("la_done")
        copied = sem("copied")
        made = sem("made")
        q_half, q_made = sem("q_half"), sem("q_made")
        z_made = sem("z_made")
        a_used = sem("a_used")
        bc_used = sem("bc_used")
        acc_evac = sem("acc_evac")
        rows_in = sem("rows_in")
        srcf_made, same_made, prior_made = sem("srcf_made"), sem("same_made"), sem("prior_made")
        idx_step = sem("idx_step")
        sidx_made = sem("sidx_made")
        scattered = sem("scattered")
        nx_in = [sem(f"nx_in{b}") for b in range(3)]
        na_in = [sem(f"na_in{b}") for b in range(3)]
        n_lin = sem("n_lin")
        n_sum = sem("n_sum")
        n_stats, n_aggr, n_mv, n_sd = sem("n_stats"), sem("n_aggr"), sem("n_mv"), sem("n_sd")
        n_step, n_rs0, n_rs = sem("n_step"), sem("n_rs0"), sem("n_rs")
        n_norm = sem("n_norm")
        n_out = [sem(f"n_out{b}") for b in range(3)]

        NCONST = 7 * 16
        NZERO = N // (P * ZR)
        NSCALE = 13
        srcT_rows = srcT.rearrange("(t j) p -> t j p", j=J)
        block = ctx.enter_context(nc.Block())

        @block.sync
        def _(sp):
            for d, s in ((sel[:, :, :].rearrange("p a b -> p (a b)"), c_sel), (eyeb[:, :], c_eyeb), (eye[:, :], c_eye),
                         (fold[:, :], c_fold), (sum4[:, :], c_sum4), (earlier[:, :], c_earlier), (dump[:, :], c_dump)):
                sp.dma_start(d, s).then_inc(consts_in, 16)
            sp.dma_start(dst_all[:, 0:COLS], dst).then_inc(tables_in, 16)
            sp.dma_start(src_all[:, 0:COLS], src).then_inc(tables_in, 16)
            sp.dma_start(attr_all[:, :], attr).then_inc(tables_in, 16)
            sp.wait_ge(small_zeroed, 6)
            sp.dma_start(wa[0:64, 0:64], wm000.rearrange("u a w -> u (a w)")).then_inc(weights_in, 16)
            sp.dma_start(wa[64:128, 0:64], lm0).then_inc(weights_in, 16)
            sp.dma_start(wa[64:128, C:C + F1], wm011.rearrange("u a w -> u (a w)")).then_inc(weights_in, 16)
            for k in range(3):
                col = F0 + F1 * k
                sp.dma_start(wb[32 * k:32 * k + 32, 32 * k:32 * k + 32], lm1).then_inc(weights_in, 16)
                sp.dma_start(wc[32 * k:32 * k + 32, col:col + F1],
                             wm101.rearrange("u a w -> u (a w)")).then_inc(weights_in, 16)
            sp.dma_start(wc[96:128, 0:64], wm110.rearrange("u a w -> u (a w)")).then_inc(weights_in, 16)
            sp.dma_start(wl0[0:64, 0:64], lu0).then_inc(weights_in, 16)
            sp.dma_start(wl0[64:96, 64:96], lu1).then_inc(weights_in, 16)
            sp.dma_start(wl0[96:128, 96:128], lu1).then_inc(weights_in, 16)
            sp.dma_start(wl1[0:32, 128:160], lu1).then_inc(weights_in, 16)
            sp.dma_start(w000[:, :, :], wu000.rearrange("u v w -> (u v) w").rearrange("(c p) w -> p c w", p=128)
                         ).then_inc(weights_in, 16)
            sp.dma_start(w110[:, :, :], wu110.rearrange("u v w -> (u v) w").rearrange("(c p) w -> p c w", p=128)
                         ).then_inc(weights_in, 16)
            sp.dma_start(wt[64:128, 0:GB, :].rearrange("p c (i w) -> p (c i) w", w=F1),
                         wu101.rearrange("u v w -> v u w")).then_inc(weights_in, 16)
            sp.dma_start(wt[0:64, GB:2 * GB, :].rearrange("p c w -> p (c w)"),
                         wu011.rearrange("u v w -> u (v w)")).then_inc(weights_in, 16)
            sp.wait_ge(zeros_made, 1)
            for n in range(NZERO):
                sp.dma_start(acc[n * P * ZR:(n + 1) * P * ZR, :].rearrange("(p a r) c -> p a (r c)", p=P, r=2),
                             zeros[:, :, :].to_broadcast((P, ZR // 2, 2 * C))).then_inc(acc_zeroed, 16)
            sp.dma_start(acc[N:N + DUMP, :], zeros[:, 0, 0:C]).then_inc(acc_zeroed, 16)

            def load_rows(t, first=False):
                if not first:
                    sp.wait_ge(same_made, t)
                sp.dma_start(rows[:, :, :], srcT_rows[t, :, :].rearrange("(a j) p -> a j p", a=1)
                             .to_broadcast((P, J, P))).then_inc(rows_in, 16)

            load_rows(0, first=True)
            with sp.Fori(1, TILES) as t:
                load_rows(t)

            def node_loads(n, b):
                sp.dma_start(xa[:, b, :], xT[0:128, bass.ds(n * T, T)]).then_inc(nx_in[b], 16)
                sp.dma_start(xb[0:32, b, :], xT[128:160, bass.ds(n * T, T)]).then_inc(nx_in[b], 16)
                sp.dma_start(ya[:, b, :], acc[bass.ds(n * T, T), :].rearrange("(p j) c -> p (j c)", p=P)
                             ).then_inc(na_in[b], 16)

            def node_store(n, b):
                sp.wait_ge(n_norm, n + 1)
                sp.dma_start(out[bass.ds(n * T, T), :].rearrange("(p j) c -> p (j c)", p=P), yo[:, b, :]
                             ).then_inc(n_out[b], 16)

            sp.wait_ge(small_zeroed, 7)
            sp.wait_ge(scattered, 16 * J * TILES)
            for n in range(3):
                node_loads(n, n)
            with sp.Fori(1, NT // 3) as i:
                for b in range(3):
                    node_store(3 * i + (b - 3), b)
                    node_loads(3 * i + b, b)
            node_store(NT - 4, 0)
            node_loads(NT - 1, 0)
            for n in range(NT - 3, NT):
                node_store(n, n % 3)
            for b in range(3):
                sp.wait_ge(n_out[b], 16 * ((NT - b + 2) // 3))

        @block.gpsimd
        def _(pool):
            pool.memset(wa[:, :], 0.0).then_inc(small_zeroed, 1)
            pool.memset(wb[:, :], 0.0).then_inc(small_zeroed, 1)
            pool.memset(wc[:, :], 0.0).then_inc(small_zeroed, 1)
            pool.memset(wl0[:, :], 0.0).then_inc(small_zeroed, 1)
            pool.memset(wl1[:, :], 0.0).then_inc(small_zeroed, 1)
            pool.memset(wt[:, :, :], 0.0).then_inc(small_zeroed, 1)
            pool.memset(dst_all[:, COLS:COLS + J], 0.0)
            pool.memset(src_all[:, COLS:COLS + J], 0.0)
            pool.wait_ge(tables_in, 48)

            def gather_start(f, pos=None):
                if pos:
                    pool.wait_ge(xi_in, f * 64)
                    pool.wait_ge(xj_in, f * 64)
                pool.tensor_copy(dcur[:, :], dst_all[:, bass.ds(f * J, J)]).then_inc(idx_cur, 1)
                pool.tensor_copy(scur[:, :], src_all[:, bass.ds(f * J, J)]).then_inc(idx_cur, 1)
                pool.wait_ge(idx_cur, f * 2 + 2)
                if pos:
                    pool.wait_ge(aux_evac, pos.after("ft2"))
                    pool.wait_ge(rx_done, f)
                pool.sem_inc(parted, 1)

            def gather(j):
                pool.indirect_dma_start(G[:, j, F0:F0 + C], None, x,
                                        bass.IndirectOffsetOnAxis(ap=dcur[:, j:j + 1], axis=0)).then_inc(xj_in, 16)
                pool.indirect_dma_start(XI[:, j, :], None, x,
                                        bass.IndirectOffsetOnAxis(ap=scur[:, j:j + 1], axis=0)).then_inc(xi_in, 16)

            def features(f):
                pool.wait_ge(xj_in, f * 64 + 64)
                pool.wait_ge(attr_cur, f + 1)
                e0 = acur[:, :, 3:4]
                pool.tensor_tensor(G[:, :, 0:F0], G[:, :, F0:2 * F0], e0.to_broadcast((P, J, F0)), ALU.mult
                                   ).then_inc(feat_pool, 1)
                pool.tensor_tensor(H[:, :, 0:96], G[:, :, 2 * F0:F0 + C], e0.to_broadcast((P, J, 96)), ALU.mult
                                   ).then_inc(feat_pool, 1)

            def scatter(b, j, pos, first=False):
                pool.wait_ge(aux_evac, pos.after(f"ud{j // 2}"))
                pool.wait_ge(sidx_made, b + 1)
                if not (first and j == 0):
                    pool.wait_ge(scattered, b * 64 + 16 * j)
                pool.sem_inc(parted, 1)
                pool.indirect_dma_start(acc, bass.IndirectOffsetOnAxis(ap=sidx[:, j:j + 1], axis=0), UD[:, j, :], None,
                                        compute_op=ALU.add).then_inc(scattered, 16)

            def body(t, par, back, front):
                pos = body_pos(t, back, front)

                def product(s, name):
                    pool.wait_ge(made, t * NV + v_after(s, name))

                def add_bc(s, k):
                    if k in ADDS[s]:
                        product(s, "C01" if k < 2 else "C2")
                        pool.tensor_tensor(ZB[:, s % 4, k, :], ZB[:, s % 4, k, :], ZC[:, s % 4, k, :], ALU.add
                                           ).then_inc(z_made, 1)

                for s in range(SLOTS):
                    if front and s == 0:
                        features(t + 1)
                    product(s, "P01")
                    if s >= 2 or back:
                        pool.wait_ge(bc_used, t * GB + (s - 1))
                    pool.tensor_tensor(QB[:, s % 2, :], PB[:, s % 2, 0, :], PB[:, s % 2, 1, :], ALU.add
                                       ).then_inc(q_half, 1)
                    add_bc(s, 0)
                    if back and s >= 6:
                        scatter(t - 1, 2 * (s - 6), pos, isinstance(t, int) and t == 1)
                    add_bc(s, 1)
                    product(s, "P2")
                    pool.wait_ge(q_half, t * GB + (s + 1))
                    pool.tensor_tensor(QB[:, s % 2, :], QB[:, s % 2, :], PB[:, s % 2, 2, :], ALU.add
                                       ).then_inc(q_made, 1)
                    add_bc(s, 2)
                    if back and s >= 6:
                        scatter(t - 1, 2 * (s - 6) + 1, pos)
                    if front and GATHER_SLOT <= s < GATHER_SLOT + J:
                        if s == GATHER_SLOT:
                            gather_start(t + 2, pos)
                        gather(s - GATHER_SLOT)

            gather_start(0)
            for j in range(J):
                gather(j)
            features(0)
            gather_start(1, prologue_pos())
            for j in range(J):
                gather(j)
            body(0, 0, False, True)
            pool.wait_ge(acc_zeroed, 16 * (NZERO + 1))
            with pool.Fori(0, (TILES - 2) // 2) as i:
                body(2 * i + 1, 1, True, True)
                body(2 * i + 2, 0, True, True)
            body(TILES - 1, 1, True, False)
            tail = tail_pos()
            for j in range(J):
                scatter(TILES - 1, j, tail)
            pool.wait_ge(xj_in, 64 * (TILES + 1))
            pool.wait_ge(xi_in, 64 * (TILES + 1))
            pool.wait_ge(bc_used, TILES * GB)
            pool.wait_ge(a_used, TILES * GA)
            pool.memset(xb, 0.0).then_inc(small_zeroed, 1)

        @block.scalar
        def _(act):
            copy = ACT.Copy

            act.wait_ge(weights_in, 16 * 18)
            r96 = 96.0 ** -0.5
            for ap, s in ((wa[0:64, 0:64], r96), (wa[64:128, 0:64], 0.125), (wa[64:128, C:C + F1], r96),
                          (wb[:, :], 32.0 ** -0.5), (wc[0:96, :], r96), (wc[96:128, :], (3.0 * 96.0) ** -0.5),
                          (wl0[0:64, :], 0.125), (wl0[64:128, :], 32.0 ** -0.5), (wl1[:, :], 32.0 ** -0.5),
                          (w000[:, :, :], 5120.0 ** -0.5), (w110[:, :, :], (3.0 * 5120.0) ** -0.5),
                          (wt[64:128, 0:GB, :], 1.0 / 64), (wt[0:64, GB:2 * GB, :], 1.0 / 64)):
                act.activation(ap, ap, copy, scale=s).then_inc(weights_ready, 1)

            def evac(dst_ap, pos, name, ps):
                act.wait_ge(aux_ready, pos.after(name))
                act.activation(dst_ap, ps, copy).then_inc(aux_evac, 1)

            def bank(pos, name):
                return aux[pos.bank(name)]

            def part(S, p):
                return S[:, :, :, p, :].rearrange("p j b f -> p (j b) f")

            def flat(a):
                return a[:, :, :].rearrange("p j (b f) -> p (j b) f", f=32)

            def front_piece(name, par, pos):
                ps = bank(pos, name)
                n = int(name[-1])
                if name.startswith("ft"):
                    r = 96 if n == 1 else 128
                    evac(FT[0:r, n, :], pos, name, ps[0:r, 0:T])
                elif name.startswith("m"):
                    evac(M[:, 2 * n:2 * n + 2, :], pos, name,
                         ps[0:P, 0:2 * (C + F1)].rearrange("p (j c) -> p j c", j=2))
                elif name.startswith("sx"):
                    evac(ST[:, par, n, :], pos, name, ps[0:96, 0:T])
                elif name.startswith("sa"):
                    evac(ST[:, par, 5 + n, :], pos, name, ps[0:96, 0:T])
                else:
                    evac(REP[:, par, n, :], pos, name, ps[:, 0:T])

            def split_x(f, step):
                if step == 0:
                    act.wait_ge(xi_in, (f + 1) * 64)
                    act.activation(part(SX, 0), flat(XI), copy).then_inc(hx_done, 1)
                else:
                    act.wait_ge(rx_done, f + 1)
                    act.activation(part(SX, 1), flat(R), copy).then_inc(mx_done, 1)

            def split_a(f, step):
                if step == 0:
                    act.wait_ge(msg_done, f + 1)
                    act.activation(SA[:, :, :, 0, :], M[:, :, 0:C].rearrange("p j (b f) -> p j b f", f=32), copy
                                   ).then_inc(ha_done, 1)
                else:
                    act.wait_ge(ra_done, f + 1)
                    act.activation(part(SA, 1), flat(R), copy).then_inc(ma_done, 1)

            def acc_out(b):
                act.wait_ge(bc_used, (b + 1) * GB)
                act.wait_ge(a_used, (b + 1) * GA)
                act.activation(U0[:, :], acc0[:, 0:T], copy).then_inc(acc_evac, 1)
                act.activation(U1[:, :], acc1[0:96, 0:T], copy).then_inc(acc_evac, 1)

            def back_piece(name, b, pos, first=False):
                n = int(name[-1])
                if name == "ud0" and not first:
                    act.wait_ge(scattered, b * 64)
                evac((UL if name[1] == "l" else UD)[:, 2 * n:2 * n + 2, :], pos, name,
                     bank(pos, name)[0:P, 0:2 * C].rearrange("p (j c) -> p j c", j=2))

            def body(t, par, back, front):
                pos = body_pos(t, back, front)

                def pieces(s, point):
                    if back:
                        for name in BACK_AT.get((s, point), []):
                            back_piece(name, t - 1, pos, isinstance(t, int) and t == 1)
                    if front:
                        for name in FRONT_AT.get((s, point), []):
                            front_piece(name, 1 - par, pos)

                for s in range(SLOTS):
                    for point in range(5):
                        for name in T_AT.get((s, point), []):
                            u = int(name[-1])
                            if u >= 2:
                                act.wait_ge(made, t * NV + v_after(u - 2, "C2"))
                            evac(TS[:, 2 * (u % 2) + (name[1] == "0"), :], pos, name, bank(pos, name)[:, 0:T])
                        pieces(s, point)
                        if front and (s, point) in ((0, 0), (1, 2)):
                            split_x(t + 1, s)
                        if front and (s, point) in ((4, 2), (5, 2)):
                            split_a(t + 1, s - 4)
                        if back and (s, point) == (0, 3):
                            acc_out(t - 1)

            pro = prologue_pos()
            split_x(0, 0)
            split_x(0, 1)
            for name in FRONT:
                if name == "sa0":
                    split_a(0, 0)
                    split_a(0, 1)
                front_piece(name, 0, pro)
            body(0, 0, False, True)
            with act.Fori(0, (TILES - 2) // 2) as i:
                body(2 * i + 1, 1, True, True)
                body(2 * i + 2, 0, True, True)
            body(TILES - 1, 1, True, False)
            tail = tail_pos()
            acc_out(TILES - 1)
            for name in ("ul0", "ul1", "ud0", "ud1"):
                back_piece(name, TILES - 1, tail)

            def node_sd(n, b):
                act.wait_ge(n_mv, n + 1)
                act.activation(sd[:, b, :], ve[:, b, :], ACT.Sqrt).then_inc(n_sd, 1)

            def node_norm(n, b, left):
                act.wait_ge(n_rs, n + 1)
                if left is not None:
                    act.wait_ge(n_out[b], left)
                for j in range(J):
                    last = act.activation(yo[:, b, j * C:(j + 1) * C], ya[:, b, j * C:(j + 1) * C], ACT.Identity,
                                          bias=nb[:, b, j:j + 1], scale=rs[:, b, j:j + 1])
                last.then_inc(n_norm, 1)

            for n in range(6):
                node_sd(n, n % 3)
                if n:
                    node_norm(n - 1, (n - 1) % 3, 16 if n > 3 else None)
            with act.Fori(2, NT // 3) as i:
                for b in range(3):
                    node_sd(3 * i + b, b)
                    node_norm(3 * i + (b - 1), (b - 1) % 3, (i - 1) * 16 if b == 0 else i * 16)
            n = NT - 1
            node_sd(n, n % 3)
            node_norm(n - 1, (n - 1) % 3, ((n - 1) // 3) * 16)
            node_norm(n, n % 3, (n // 3) * 16)

        @block.vector
        def _(dve):
            def part(S, p):
                return S[:, :, :, p, :].rearrange("p j b f -> p (j b) f")

            def flat(a):
                return a[:, :, :].rearrange("p j (b f) -> p (j b) f", f=32)

            def load_attr(f, first=False):
                if not first:
                    dve.wait_ge(feat_pool, f * 2)
                dve.tensor_copy(acur[:, :, :].rearrange("p j a -> p (j a)"), attr_all[:, bass.ds(f * (4 * J), 4 * J)]
                                ).then_inc(attr_cur, 1)

            def dot_r(f):
                dve.wait_ge(xj_in, (f + 1) * 64)
                dve.wait_ge(attr_cur, f + 1)
                r = acur[:, :, 0:3].rearrange("p j (k a) -> p j k a", a=1).to_broadcast((P, J, 3, F1))
                dve.tensor_tensor(rx1[:, :, :, :], G[:, :, 2 * F0:F0 + C].rearrange("p j (k u) -> p j k u", k=3), r,
                                  ALU.mult).then_inc(rx1_made, 1)
                dve.wait_ge(rx1_made, f + 1)
                dve.tensor_reduce(H[:, :, 96:128], rx1[:, :, :, :].rearrange("p j k u -> p j u k"), AX.X, ALU.add
                                  ).then_inc(feat_dve, 1)

            def message(f, pos):
                dve.wait_ge(aux_evac, pos.after("m1"))
                z = M[:, :, C:C + F1].rearrange("p j (a w) -> p j a w", a=1).to_broadcast((P, J, 3, F1))
                r = acur[:, :, 0:3].rearrange("p j (k a) -> p j k a", a=1).to_broadcast((P, J, 3, F1))
                dve.tensor_tensor(rz[:, :, :, :], z, r, ALU.mult).then_inc(rz_made, 1)
                dve.wait_ge(rz_made, f + 1)
                a1 = M[:, :, F0:C]
                dve.tensor_tensor(a1, a1, rz[:, :, :, :].rearrange("p j k w -> p j (k w)"), ALU.add
                                  ).then_inc(msg_done, 1)

            def rest_x(f, step):
                if step == 0:
                    dve.wait_ge(hx_done, f + 1)
                    dve.tensor_tensor(flat(R), flat(XI), part(SX, 0), ALU.subtract).then_inc(rx_done, 1)
                else:
                    dve.wait_ge(mx_done, f + 1)
                    dve.tensor_tensor(part(SX, 2), flat(R), part(SX, 1), ALU.subtract).then_inc(lx_done, 1)

            def rest_a(f, step):
                if step == 0:
                    dve.wait_ge(ha_done, f + 1)
                    dve.tensor_tensor(R[:, :, :].rearrange("p j (b f) -> p j b f", f=32),
                                      M[:, :, 0:C].rearrange("p j (b f) -> p j b f", f=32), SA[:, :, :, 0, :],
                                      ALU.subtract).then_inc(ra_done, 1)
                else:
                    dve.wait_ge(ma_done, f + 1)
                    dve.tensor_tensor(part(SA, 2), flat(R), part(SA, 1), ALU.subtract).then_inc(la_done, 1)

            def repeats(b, step, first=False):
                if step == 0:
                    dve.tensor_copy(srcf[:, :], src_all[:, bass.ds(b * J, J)]).then_inc(srcf_made, 1)
                    dve.wait_ge(srcf_made, b + 1)
                    dve.wait_ge(rows_in, (b + 1) * 16)
                    dve.tensor_tensor(same[:, :, :], rows[:, :, :],
                                      srcf[:, :].rearrange("p (j a) -> p j a", a=1).to_broadcast((P, J, P)),
                                      ALU.is_equal).then_inc(same_made, 1)
                elif step == 1:
                    dve.wait_ge(same_made, b + 1)
                    dve.tensor_tensor(prior[:, :, :], same[:, :, :],
                                      earlier[:, :].rearrange("p (a e) -> p a e", a=1).to_broadcast((P, J, P)),
                                      ALU.mult).then_inc(prior_made, 1)
                    dve.wait_ge(prior_made, b + 1)
                    dve.tensor_reduce(dup[:, :], prior[:, :, :], AX.X, ALU.add).then_inc(idx_step, 1)
                else:
                    dve.tensor_scalar(todump[:, :], srcf[:, :], -1.0, dump[:, 0:1], ALU.mult, ALU.add
                                      ).then_inc(idx_step, 1)
                    dve.wait_ge(idx_step, b * 4 + 2)
                    dve.tensor_scalar(dup[:, :], dup[:, :], 1.0, None, ALU.min).then_inc(idx_step, 1)
                    dve.wait_ge(idx_step, b * 4 + 3)
                    dve.tensor_tensor(todump[:, :], todump[:, :], dup[:, :], ALU.mult).then_inc(idx_step, 1)
                    dve.wait_ge(idx_step, b * 4 + 4)
                    if not first:
                        dve.wait_ge(scattered, b * 64)
                    dve.tensor_tensor(sidx[:, :], todump[:, :], srcf[:, :], ALU.add).then_inc(sidx_made, 1)

            def body(t, par, back, front):
                pos = body_pos(t, back, front)
                def replicated(n):
                    if isinstance(t, int) and t == 0:
                        dve.wait_ge(aux_evac, len(FRONT) - n)
                    else:
                        dve.wait_ge(aux_evac, pos.start() - n)


                def copied_in(s, name):
                    n = copy_use(s, name)
                    dve.wait_ge(copied, t * NX + (n + 1))
                    return 2 * (n % 2)

                def twice(a):
                    return a.rearrange("p (a e) -> p a e", a=1).to_broadcast((128, 2, T))

                def multiply(o, i0, i1):
                    dve.tensor_tensor(o, i0, i1, ALU.mult).then_inc(made, 1)

                for s in range(SLOTS):
                    h, z = s % 2, s % 4
                    t101, t011 = TS[:, 2 * h, :], TS[:, 2 * h + 1, :]
                    if s >= 2 or back:
                        dve.wait_ge(a_used, t * GA + (s - 1))
                    if s == 0:
                        replicated(3)
                    b = copied_in(s, "A01")
                    multiply(PA[:, 4 * h:4 * h + 2, :], copies[:, b:b + 2, 0:T], twice(REP[:, par, 0, :]))
                    if front:
                        f = t + 1
                        if s == 0:
                            load_attr(f)
                            dot_r(f)
                        if s in (1, 2):
                            rest_x(f, s - 1)
                        if s == 4:
                            message(f, pos)
                    if s >= 2 or back:
                        dve.wait_ge(q_made, t * GB + (s - 1))
                    if s == 0:
                        replicated(1)
                    b = copied_in(s, "X01")
                    multiply(PB[:, h, 0:2, :], copies[:, b:b + 2, 0:T], REP[:, par, 1:3, :])
                    dve.wait_ge(aux_evac, pos.after(f"t101_{s}"))
                    if s >= 4 or back:
                        dve.wait_ge(bc_used, t * GB + (s - 3))
                    multiply(ZB[:, z, 0:2, :], copies[:, b:b + 2, 0:T], twice(t101))
                    dve.wait_ge(aux_evac, pos.after(f"t011_{s}"))
                    b = copied_in(s, "V01")
                    multiply(ZC[:, z, 0:2, :], copies[:, b:b + 2, 0:T], twice(t011))
                    b = copied_in(s, "A23")
                    multiply(PA[:, 4 * h + 2:4 * h + 4, :], copies[:, b:b + 2, 0:T], twice(REP[:, par, 0, :]))
                    if s == 0:
                        replicated(0)
                    b = copied_in(s, "XV2")
                    multiply(PB[:, h, 2, :], copies[:, b, 0:T], REP[:, par, 3, :])
                    multiply(ZB[:, z, 2, :], copies[:, b, 0:T], t101)
                    multiply(ZC[:, z, 2, :], copies[:, b + 1, 0:T], t011)
                    if front and s in (4, 5):
                        rest_a(f, s - 4)
                    if back and 3 <= s < 6:
                        repeats(t - 1, s - 3, isinstance(t, int) and t == 1)

            dve.memset(zeros[:, :, :], 0.0).then_inc(zeros_made, 1)
            dve.wait_ge(weights_ready, NSCALE)
            dve.wait_ge(consts_in, NCONST)
            dve.scalar_tensor_tensor(wl0[:, 0:128], eye[:, :], 2.0, wl0[:, 0:128], ALU.mult, ALU.add
                                     ).then_inc(wl_ready, 1)
            dve.scalar_tensor_tensor(wl1[0:32, 128:160], eye[0:32, 0:32], 2.0, wl1[0:32, 128:160], ALU.mult, ALU.add
                                     ).then_inc(wl_ready, 1)
            dve.wait_ge(tables_in, 48)
            pro = prologue_pos()
            load_attr(0, first=True)
            dot_r(0)
            rest_x(0, 0)
            rest_x(0, 1)
            message(0, pro)
            rest_a(0, 0)
            rest_a(0, 1)
            body(0, 0, False, True)
            with dve.Fori(0, (TILES - 2) // 2) as i:
                body(2 * i + 1, 1, True, True)
                body(2 * i + 2, 0, True, True)
            body(TILES - 1, 1, True, False)
            for step in range(3):
                repeats(TILES - 1, step)

            def node_stats(n, b, group):
                dve.wait_ge(n_lin, n + 1)
                dve.wait_ge(na_in[b], (group + 1) * 16)
                for h in range(2):
                    y = ya[:, b, 2 * C * h:2 * C * (h + 1)]
                    dve.tensor_tensor(y, pairs[b][h][0:P, 0:2 * C], y, ALU.add).then_inc(n_sum, 1)
                dve.wait_ge(n_sum, (n + 1) * 2)
                for j in range(J):
                    last = dve.bn_stats(stats[:, b, j, :], ya[:, b, j * C:(j + 1) * C])
                last.then_inc(n_stats, 1)
                dve.wait_ge(n_stats, n + 1)
                dve.sem_inc(parted_v, 1)
                for j in range(J):
                    last = dve.bn_aggr(mv[:, b, j, :], stats[:, b, j, :])
                last.then_inc(n_aggr, 1)
                dve.wait_ge(n_aggr, n + 1)
                dve.tensor_scalar(ve[:, b, :], mv[:, b, :, 1], EPS, None, ALU.add).then_inc(n_mv, 1)

            def node_scale(n, b):
                dve.wait_ge(n_sd, n + 1)
                dve.reciprocal(r0[:, b, :], sd[:, b, :]).then_inc(n_step, 1)
                dve.wait_ge(n_step, n * 4 + 1)
                dve.tensor_tensor(hv[:, b, :], r0[:, b, :], r0[:, b, :], ALU.mult).then_inc(n_step, 1)
                dve.wait_ge(n_step, n * 4 + 2)
                dve.tensor_tensor(hv[:, b, :], hv[:, b, :], ve[:, b, :], ALU.mult).then_inc(n_step, 1)
                dve.wait_ge(n_step, n * 4 + 3)
                dve.tensor_scalar(hv[:, b, :], hv[:, b, :], -0.5, 1.5, ALU.mult, ALU.add).then_inc(n_step, 1)
                dve.wait_ge(n_step, n * 4 + 4)
                dve.tensor_tensor(rs[:, b, :], r0[:, b, :], hv[:, b, :], ALU.mult).then_inc(n_rs0, 1)
                dve.wait_ge(n_rs0, n + 1)
                dve.scalar_tensor_tensor(nb[:, b, :], mv[:, b, :, 0], -1.0, rs[:, b, :], ALU.mult, ALU.mult
                                         ).then_inc(n_rs, 1)

            for n in range(3):
                node_stats(n, n, 0)
                if n:
                    node_scale(n - 1, n - 1)
            with dve.Fori(1, NT // 3) as i:
                for b in range(3):
                    node_stats(3 * i + b, b, i)
                    node_scale(3 * i + (b - 1), (b - 1) % 3)
            n = NT - 1
            node_stats(n, n % 3, n // 3)
            node_scale(n - 1, (n - 1) % 3)
            node_scale(n, n % 3)

        @block.tensor
        def _(pe):
            def aux_bank(pos, name):
                after = pos.after(name)
                if not (isinstance(after, int) and after <= 2):
                    pe.wait_ge(aux_evac, after - 2)
                return aux[pos.bank(name)]

            def front_piece(name, f, par, pos):
                n = int(name[-1])
                if name == "ft0":
                    pe.wait_ge(feat_pool, f * 2 + 2)
                    pe.wait_ge(feat_dve, f + 1)
                elif name == "m0":
                    pe.wait_ge(aux_evac, pos.after("ft2"))
                elif name == "sx0":
                    pe.wait_ge(lx_done, f + 1)
                elif name == "sa0":
                    pe.wait_ge(la_done, f + 1)
                elif name == "rep4":
                    pe.wait_ge(aux_evac, pos.after("sa4"))
                ps = aux_bank(pos, name)
                if name.startswith("ft"):
                    for j in range(J):
                        f_in = (G[:, j, 0:128], G[:, j, 128:224], H[:, j, :])[n]
                        m = 96 if n == 1 else 128
                        last = pe.matmul(ps[0:m, j * P:(j + 1) * P], f_in, eye[0:P, 0:P], start=True, stop=True)
                elif name.startswith("m"):
                    for jj in range(2):
                        e = slice((2 * n + jj) * P, (2 * n + jj + 1) * P)
                        o = jj * (C + F1)
                        pe.matmul(ps[0:P, o:o + C + F1], FT[:, 0, e], wa[:, :], start=True, stop=False)
                        pe.matmul(ps[0:P, o + F0:o + C], FT[0:96, 1, e], wb[:, :], start=False, stop=False)
                        last = pe.matmul(ps[0:P, o:o + C], FT[:, 2, e], wc[:, :], start=False, stop=True)
                elif name.startswith("s"):
                    S = SX if name[1] == "x" else SA
                    for j in range(J):
                        last = pe.matmul(ps[0:96, j * P:(j + 1) * P], S[:, j, n, :, :].rearrange("p a f -> p (a f)"),
                                         eyeb[0:P, 0:P], start=True, stop=True)
                elif n == 0:
                    for b in range(2):
                        last = pe.matmul(ps[:, 0:T], sel[:, REPA + b, :], ST[:, par, 5 + b, :],
                                         start=(b == 0), stop=(b == 1))
                elif n < 4:
                    last = pe.matmul(ps[:, 0:T], sel[:, REP4, :], ST[:, par, 6 + n, :], start=True, stop=True)
                else:
                    for q, b in enumerate((0, 1, 5, 6)):
                        last = pe.matmul(ps[:, 0:T], sel[:, STK + q, :], ST[:, par, b, :],
                                         start=(q == 0), stop=(q == 3))
                last.then_inc(aux_ready, 1)

            def back_piece(name, b, pos):
                n = int(name[-1])
                if name == "ul0":
                    pe.wait_ge(acc_evac, b * 2 + 2)
                elif name == "ud0":
                    pe.wait_ge(same_made, b + 1)
                    pe.wait_ge(aux_evac, pos.after("ul1"))
                ps = aux_bank(pos, name)
                for jj in range(2):
                    j, o = 2 * n + jj, jj * C
                    if name[1] == "l":
                        pe.matmul(ps[0:P, o:o + F0], U0[:, j * P:(j + 1) * P], fold[:, :], start=True, stop=True)
                        last = pe.matmul(ps[0:P, o + F0:o + C], U1[:, j * P:(j + 1) * P], eye[0:96, 0:96],
                                         start=True, stop=True)
                    else:
                        last = pe.matmul(ps[0:P, o:o + C], same[:, j, :], UL[:, j, :], start=True, stop=True)
                last.then_inc(aux_ready, 1)

            def copy_pair(t, par, back, s, name):
                n = copy_use(s, name)
                if n >= 2:
                    q, r = divmod(n - 2, len(COPIES))
                    pe.wait_ge(made, t * NV + v_after(q, FREES[COPIES[r]]))
                elif back:
                    pe.wait_ge(made, t * NV + (v_after(SLOTS - 1, FREES[COPIES[n - 2]]) - NV))
                for i in range(2):
                    if name[0] == "A":
                        c = 4 * s + int(name[1]) + i
                        lhsT, rhs = sel[:, SEL2 + c % 16, :], ST[:, par, c // 16, :]
                    else:
                        stack = {"X01": 2 + i, "V01": 7 + i, "XV2": 4 + 5 * i}[name]
                        lhsT, rhs = sel[:, SEL4 + s, :], ST[:, par, stack, :]
                    last = pe.matmul(copies[:, 2 * (n % 2) + i, 0:T], lhsT, rhs, start=True, stop=True)
                last.then_inc(copied, 1)

            def contract_a(t, s, pair):
                pe.wait_ge(made, t * NV + v_after(s, ("A01", "A23")[pair]))
                for i in (2 * pair, 2 * pair + 1):
                    c = 4 * s + i
                    h = 64 * (c % 2)
                    last = pe.matmul(acc0[h:h + 64, 0:T], w000[:, c, :], PA[:, c % 8, :],
                                     start=(c < 2), stop=(c >= NA - 2))
                if pair:
                    last.then_inc(a_used, 1)

            def contract_bc(t, s):
                h = 64 * (s % 2)
                pe.wait_ge(q_made, t * GB + (s + 1))
                pe.matmul(acc0[h:h + 64, 0:T], w110[:, s, :], QB[:, s % 2, :], start=False, stop=False)
                for k in range(3):
                    o, stop = acc1[32 * k:32 * k + 32, 0:T], s == SLOTS - 1
                    if k in ADDS[s]:
                        pe.wait_ge(z_made, t * NZ + z_after(s, k))
                    else:
                        pe.wait_ge(made, t * NV + v_after(s, "C2"))
                        pe.matmul(o, sum4[:, :], ZC[:, s % 4, k, :], start=(s == 0), stop=False)
                    last = pe.matmul(o, sum4[:, :], ZB[:, s % 4, k, :], start=(s == 0 and k in ADDS[s]), stop=stop)
                last.then_inc(bc_used, 1)

            def body(t, par, back, front):
                pos = body_pos(t, back, front)
                if isinstance(t, int) and t == 0:
                    pe.wait_ge(aux_evac, prologue_pos().after("rep4"))
                else:
                    pe.wait_ge(aux_evac, pos.start() - 4)
                assert FRONT[-5] == "rep4"

                def pieces(s, point):
                    for name in T_AT.get((s, point), []):
                        w = int(name[-1]) + (GB if name[1] == "0" else 0)
                        ps = aux_bank(pos, name)
                        pe.matmul(ps[:, 0:T], wt[:, w, :], REP[:, par, 4, :], start=True, stop=True
                                  ).then_inc(aux_ready, 1)
                    if back:
                        for name in BACK_AT.get((s, point), []):
                            back_piece(name, t - 1, pos)
                    if front:
                        for name in FRONT_AT.get((s, point), []):
                            front_piece(name, t + 1, 1 - par, pos)


                for s in range(SLOTS):
                    u, v = (t, s - 1) if s else (t - 1, SLOTS - 1)
                    lagging = s > 0 or back

                    copy_pair(t, par, back, s, "A01")
                    pieces(s, 0)
                    copy_pair(t, par, back, s, "X01")
                    if s == 1 and back:
                        pe.wait_ge(acc_evac, t * 2)
                    if lagging:
                        contract_a(u, v, 0)
                    pieces(s, 1)
                    copy_pair(t, par, back, s, "V01")
                    if lagging:
                        contract_bc(u, v)
                    pieces(s, 2)
                    copy_pair(t, par, back, s, "A23")
                    if lagging:
                        contract_a(u, v, 1)
                    pieces(s, 3)
                    copy_pair(t, par, back, s, "XV2")
                    pieces(s, 4)

            pe.wait_ge(consts_in, NCONST)
            pe.wait_ge(weights_ready, NSCALE)
            pro = prologue_pos()
            for name in FRONT:
                front_piece(name, 0, 0, pro)
            body(0, 0, False, True)
            with pe.Fori(0, (TILES - 2) // 2) as i:
                body(2 * i + 1, 1, True, True)
                body(2 * i + 2, 0, True, True)
            body(TILES - 1, 1, True, False)
            contract_a(TILES - 1, SLOTS - 1, 0)
            contract_bc(TILES - 1, SLOTS - 1)
            contract_a(TILES - 1, SLOTS - 1, 1)
            tail = tail_pos()
            for name in ("ul0", "ul1", "ud0", "ud1"):
                back_piece(name, TILES - 1, tail)

            pe.wait_ge(wl_ready, 2)

            def node_lin(n, b, group, reuse):
                if reuse:
                    pe.wait_ge(n_sum, 2 * n - 4)
                pe.wait_ge(nx_in[b], (group + 1) * 32)
                for j in range(J):
                    ps = pairs[b][j // 2][0:P, (j % 2) * C:(j % 2 + 1) * C]
                    pe.matmul(ps, xa[:, b, j * P:(j + 1) * P], wl0[:, :], start=True, stop=False)
                    last = pe.matmul(ps, xb[:, b, j * P:(j + 1) * P], wl1[:, :], start=False, stop=True)
                last.then_inc(n_lin, 1)

            for n in range(3):
                node_lin(n, n, 0, False)
            with pe.Fori(1, NT // 3) as i:
                for b in range(3):
                    node_lin(3 * i + b, b, i, True)
            node_lin(NT - 1, (NT - 1) % 3, (NT - 1) // 3, True)


_INS = ["x", "xT", "src", "srcT", "dst", "attr", "wm000", "wm011", "wm101", "wm110", "lm0", "lm1",
        "wu000", "wu011", "wu101", "wu110", "lu0", "lu1", "c_sel", "c_eyeb", "c_eye", "c_fold", "c_sum4",
        "c_earlier", "c_dump"]


def kernel(x, src, dst, edge_attr_4, node_vec1, **w):
    import ml_dtypes
    import concourse.bacc as _bacc
    from concourse.bass_utils import run_bass_kernel_spmd as _run

    x = np.asarray(x)
    xk = np.concatenate([x[:, :F0], x[:, F0:].reshape(N, F1, 3).transpose(0, 2, 1).reshape(N, 3 * F1)], 1)
    xT = xk.reshape(NT, P, J, C).transpose(3, 0, 2, 1).reshape(C, N)
    arrays = {
        "x": xk, "xT": xT,
        "src": np.asarray(src).reshape(P, COLS), "srcT": np.asarray(src).reshape(P, COLS).T,
        "dst": np.asarray(dst).reshape(P, COLS), "attr": np.asarray(edge_attr_4).reshape(P, COLS * 4),
    }
    for name in _INS[6:18]:
        key = "L0_gnn_" + name
        arrays[name] = np.asarray(w[key])
    for name, (a, dt) in constants().items():
        arrays[name] = np.asarray(a, dtype=ml_dtypes.bfloat16 if dt == "bfloat16" else dt)
    arrays = {k + "_dram": np.ascontiguousarray(v) for k, v in arrays.items()}

    nc = _bacc.Bacc("TRN2", target_bir_lowering=False, num_devices=1)
    args = [nc.dram_tensor(n + "_dram", arrays[n + "_dram"].shape, mybir.dt.from_np(arrays[n + "_dram"].dtype),
                           kind="ExternalInput").ap() for n in _INS]
    out = nc.dram_tensor("out_dram", (N, C), mybir.dt.float32, kind="ExternalOutput").ap()
    build(nc, *args, out)
    got = _run(nc, [arrays], core_ids=[0]).results[0]["out_dram"]
    return np.concatenate([got[:, :F0], got[:, F0:].reshape(N, 3, F1).transpose(0, 2, 1).reshape(N, 3 * F1)], 1)
```

```python
import concourse.bass as bass
from concourse import mybir
from contextlib import ExitStack
import numpy as np

N, E, F0, F1, C = 50000, 25000, 64, 32, 160
P = 125
J = 4
T = P * J
TILES = E // T
COLS = E // P
JN = 8
TN = P * JN
NT = N // TN
NB = 4
NA = F0 // 2
GA = NA // 4
GB = F1 // 4
DUMP = P
ZR = 10
ZSTEP = 4
EPS = 1e-5

SEL2, SEL4, REP4, REPA = 0, 16, 24, 25
NSEL = 27


def selectors():
    k = np.arange(96)[:, None] % 32
    m = np.arange(128)[None, :]
    parts = [k == 2 * c + m // 64 for c in range(16)]
    parts += [k == 4 * c + m // 32 for c in range(8)]
    parts += [k == m % 32]
    parts += [2 * k + b == m % 64 for b in range(2)]
    return np.concatenate([np.broadcast_to(a, (96, 128)) for a in parts], 1)


def constants():
    p = np.arange(128)
    return {
        "c_sel": (selectors(), "bfloat16"),
        "c_eyeb": (np.eye(128), "bfloat16"),
        "c_eye": (np.eye(128), "float32"),
        "c_fold": (p[:, None] % 64 == np.arange(64)[None, :], "float32"),
        "c_sum4": (p[:, None] % 32 == np.arange(32)[None, :], "float32"),
        "c_earlier": (np.arange(P)[None, :] < np.arange(P)[:, None], "float32"),
        "c_dump": (N + np.arange(P)[:, None], "float32"),
    }


SLOTS = GA
BACK_AT = {(4, 0): ["ul0", "ul1"], (5, 0): ["ud0"], (5, 4): ["ud1"]}
FRONT_AT = {(0, 2): ["ft0", "ft1"], (1, 1): ["ft2"], (1, 4): ["m0"], (2, 1): ["m1"], (3, 0): ["m2"], (3, 1): ["m3"],
            (3, 2): ["sx0", "sx1"], (4, 1): ["sx2", "sx3"], (4, 4): ["sx4"], (5, 1): ["v0"], (5, 3): ["v1"],
            (6, 0): ["v2"], (6, 1): ["v3", "sa0"], (6, 2): ["sa1", "sa2"], (6, 3): ["sa3"], (7, 0): ["sa4"],
            (7, 1): ["rep0"], (7, 4): ["rep1", "rep2", "rep3"]}
T_AT = {(s, 0): [f"t101_{s}"] for s in range(SLOTS)}
T_AT |= {(s - 1, 4): [f"t011_{s}"] for s in range(1, SLOTS)}
T_AT[(0, 2)] = ["t011_0"]
FRONT = [a for at in sorted(FRONT_AT) for a in FRONT_AT[at]]
BACK = [a for at in sorted(BACK_AT) for a in BACK_AT[at]]
NBACK = len(BACK)


def aux_order(back, front):
    order = []
    for s in range(SLOTS):
        for point in range(5):
            order += T_AT.get((s, point), [])
            if back:
                order += BACK_AT.get((s, point), [])
            if front:
                order += FRONT_AT.get((s, point), [])
    return order


NAUX = len(aux_order(True, True))


class Pos:

    def __init__(self, t, par, offset, order):
        self.before, self.offset = t * NAUX, offset
        self.parity = par * NAUX + offset
        self.at = {a: n for n, a in enumerate(order)}

    def bank(self, name):
        return (self.parity + self.at[name]) % 2

    def after(self, name):
        return self.before + (self.offset + self.at[name] + 1)

    def start(self):
        return self.before + self.offset


def prologue_pos():
    return Pos(0, 0, 0, FRONT)


def body_pos(t, par, back, front):
    return Pos(t, par, len(FRONT) - (NBACK if back else 0), aux_order(back, front))


def tail_pos():
    return Pos(TILES - 1, (TILES - 1) % 2, len(FRONT) - NBACK + len(aux_order(True, False)), BACK)


COPIES = ["A01", "X01", "V01", "A23", "XV2"]
NX = SLOTS * len(COPIES)
PRODUCTS = ["A01", "P01", "B01", "C01", "A23", "P2", "B2", "C2"]
NV = SLOTS * len(PRODUCTS)
FREES = {"A01": "A01", "X01": "B01", "V01": "C01", "A23": "A23", "XV2": "C2"}
GATHER_SLOT = 2
ADDS = [(0, 1, 2) if s in (0, 1, 2) else (0, 1) for s in range(SLOTS)]
NZ = sum(len(a) for a in ADDS)


def copy_use(s, name):
    return len(COPIES) * s + COPIES.index(name)


def v_after(s, name):
    return len(PRODUCTS) * s + PRODUCTS.index(name) + 1


def z_after(s, k=None):
    return sum(len(a) for a in ADDS[:s]) + (len(ADDS[s]) if k is None else k + 1)


def build(nc, x, xT, src, srcT, dst, attr, wm000, wm011, wm101, wm110, lm0, lm1, wu000, wu011, wu101, wu110,
          lu0, lu1, c_sel, c_eyeb, c_eye, c_fold, c_sum4, c_earlier, c_dump, out):
    f32, b16, i32 = mybir.dt.float32, mybir.dt.bfloat16, mybir.dt.int32
    ALU, ACT, AX = mybir.AluOpType, mybir.ActivationFunctionType, mybir.AxisListType
    ctx = ExitStack()
    with ctx:
        def sb(name, shape, dt=f32):
            return ctx.enter_context(nc.sbuf_tensor(name, shape, dt))

        def sem(name):
            return ctx.enter_context(nc.semaphore(name))

        acc = nc.dram_tensor("acc", (N + DUMP, C), f32, kind="Internal").ap()

        sel = sb("sel", [96, NSEL, 128], b16)
        eyeb = sb("eyeb", [128, 128], b16)
        eye = sb("eye", [128, 128])
        fold = sb("fold", [128, 64])
        sum4 = sb("sum4", [128, 32])
        earlier = sb("earlier", [P, P])
        dump = sb("dump", [P, 1])
        zeros = sb("zeros", [P, 1, 2 * C])
        w000 = sb("w000", [128, NA, F0])
        w110 = sb("w110", [128, GB, F0])
        wt = sb("wt", [128, 3, 2 * GB, 128], b16)
        wa = sb("wa", [128, 96])
        wb = sb("wb", [96, 96])
        wc = sb("wc", [128, 192])
        wl0 = sb("wl0", [128, 128])
        wl1 = sb("wl1", [32, 32])
        src_all = sb("src_all", [P, COLS + J], i32)
        dst_all = sb("dst_all", [P, COLS + J], i32)
        attr_all = sb("attr_all", [P, COLS * 4])
        dcur = sb("dcur", [P, J], i32)
        scur = sb("scur", [P, J], i32)
        acur = sb("acur", [P, J, 4])
        G = sb("G", [P, J, F0 + C])
        H = sb("H", [P, J, 128])
        work = sb("work", [P, J * P])
        rx1 = work[:, 0:J * 96].rearrange("p (j k u) -> p j k u", j=J, k=3)
        prior = work[:, :].rearrange("p (j q) -> p j q", j=J)
        XI = sb("XI", [P, J, C])
        M = sb("M", [P, J, F1 + C])
        R = sb("R", [P, J, C])
        SX = sb("SX", [P, J, 3 * C], b16)
        SA = sb("SA", [P, J, 3 * C], b16)
        FT = sb("FT", [128, 3, T])
        ST = sb("ST", [96, 2, 10, T], b16)
        V = sb("V", [128, 2, 4, T], b16)
        REP = sb("REP", [128, 2, 4, T])
        arena = sb("arena", [128, 42, T])
        PA = arena[:, 0:8, :]
        PB = arena[:, 8:14, :].rearrange("p (g k) e -> p g k e", g=2)
        ZB = arena[:, 14:26, :].rearrange("p (g k) e -> p g k e", g=4)
        ZC = arena[:, 26:38, :].rearrange("p (g k) e -> p g k e", g=4)
        TS = arena[:, 38:42, :]
        flat_arena = arena[:, :, :].rearrange("p n e -> p (n e)")
        wtf = flat_arena[:, 0:2 * GB * 128].rearrange("p (c w) -> p c w", w=128)
        wtr = flat_arena[:, 2 * GB * 128:4 * GB * 128].rearrange("p (c w) -> p c w", w=128)
        QB = sb("QB", [128, 2, T])
        U0 = sb("U0", [128, T])
        U1 = sb("U1", [96, T])
        UL = sb("UL", [P, J, C])
        rows = sb("rows", [P, J, P], i32)
        srcf = sb("srcf", [P, J])
        same = sb("same", [P, J, P])
        dup = sb("dup", [P, J])
        todump = sb("todump", [P, J])
        sidx = sb("sidx", [P, J], i32)
        sizes = (TN, TN, JN * C, JN * C)
        starts = [NB * sum(sizes[:n]) for n in range(4)]
        xa, xb, ya, yo = (flat_arena[0:rows_used, o:o + NB * w].rearrange("p (b f) -> p b f", b=NB)
                          for rows_used, o, w in zip((128, 32, P, P), starts, sizes))
        tail_arena = flat_arena[0:P, starts[3] + NB * sizes[3]:]
        stats, mv, ve, sd, r0, hv, rs, nb = (
            tail_arena[:, o * NB * JN:(o + w) * NB * JN].rearrange("p (b j w) -> p b j w", b=NB, w=w)
            for o, w in ((0, 6), (6, 2), (8, 1), (9, 1), (10, 1), (11, 1), (12, 1), (13, 1)))
        ve, sd, r0, hv, rs, nb = (a[:, :, :, 0] for a in (ve, sd, r0, hv, rs, nb))

        copies = ctx.enter_context(nc.psum_tensor("copies", [128, 4, 512], f32))
        others = ctx.enter_context(nc.psum_tensor("others", [128, 4, 512], f32))
        acc0, acc1 = others[:, 0, :], others[:, 1, :]
        aux = [others[:, 2, :], others[:, 3, :]]
        quads = [copies, others]

        consts_in = sem("consts_in")
        msg_weights_in, weights_in = sem("msg_weights_in"), sem("weights_in")
        tables_in = sem("tables_in")
        small_zeroed = sem("small_zeroed")
        zeros_made = sem("zeros_made")
        acc_zeroed = sem("acc_zeroed")
        msg_weights_ready, weights_ready = sem("msg_weights_ready"), sem("weights_ready")
        wh_done, wr_done, wm_done, wl_done = sem("wh_done"), sem("wr_done"), sem("wm_done"), sem("wl_done")
        wl_ready = sem("wl_ready")
        idx_cur = sem("idx_cur")
        parted, parted_v = sem("parted"), sem("parted_v")
        attr_cur = sem("attr_cur")
        xj_in = sem("xj_in")
        xi_in = sem("xi_in")
        feat_pool = sem("feat_pool")
        rx1_made = sem("rx1_made")
        feat_dve = sem("feat_dve")
        aux_ready = sem("aux_ready")
        aux_evac = sem("aux_evac")
        rz_made = sem("rz_made")
        msg_done = sem("msg_done")
        hx_done, mx_done, ha_done, ma_done = sem("hx_done"), sem("mx_done"), sem("ha_done"), sem("ma_done")
        rx_done, lx_done, ra_done, la_done = sem("rx_done"), sem("lx_done"), sem("ra_done"), sem("la_done")
        copied = sem("copied")
        made = sem("made")
        q_half, q_made = sem("q_half"), sem("q_made")
        z_made = sem("z_made")
        a_used = sem("a_used")
        bc_used = sem("bc_used")
        acc_evac = sem("acc_evac")
        rows_in = sem("rows_in")
        srcf_made, same_made, prior_made = sem("srcf_made"), sem("same_made"), sem("prior_made")
        idx_step = sem("idx_step")
        sidx_made = sem("sidx_made")
        scattered = sem("scattered")
        nx_in = [sem(f"nx_in{b}") for b in range(NB)]
        na_in = [sem(f"na_in{b}") for b in range(NB)]
        n_lin = sem("n_lin")
        n_sum = sem("n_sum")
        n_stats, n_aggr, n_mv, n_sd = sem("n_stats"), sem("n_aggr"), sem("n_mv"), sem("n_sd")
        n_step, n_rs0, n_rs = sem("n_step"), sem("n_rs0"), sem("n_rs")
        n_norm = sem("n_norm")
        n_out = [sem(f"n_out{b}") for b in range(NB)]

        NCONST = 7 * 16
        NZERO = N // (P * ZR)
        NSCALE = 6
        srcT_rows = srcT.rearrange("(t j) p -> t j p", j=J)
        def scalars(a, first=0):
            return a[:, :, first:first + F0]

        def vectors(a, first=0):
            return a[:, :, first + F0:first + C].rearrange("p j (k f) -> p j k f", f=F1)

        def part(S, p):
            o = F0 * (1, 0, 2)[p]
            return (S[:, :, o:o + F0],
                    S[:, :, 3 * F0:].rearrange("p j (k a f) -> p j k a f", k=3, f=F1)[:, :, :, p, :])

        block = ctx.enter_context(nc.Block())

        @block.sync
        def _(sp):
            sp.dma_start(dst_all[:, 0:COLS], dst).then_inc(tables_in, 16)
            sp.dma_start(src_all[:, 0:COLS], src).then_inc(tables_in, 16)
            sp.dma_start(attr_all[:, :], attr).then_inc(tables_in, 16)
            for d, s in ((sel[:, :, :].rearrange("p a b -> p (a b)"), c_sel), (eyeb[:, :], c_eyeb), (eye[:, :], c_eye),
                         (fold[:, :], c_fold), (sum4[:, :], c_sum4), (earlier[:, :], c_earlier), (dump[:, :], c_dump)):
                sp.dma_start(d, s).then_inc(consts_in, 16)
            sp.wait_ge(small_zeroed, 4)
            sp.dma_start(wa[0:64, F1:96], wm000.rearrange("u a w -> u (a w)")).then_inc(msg_weights_in, 16)
            sp.dma_start(wa[64:128, F1:96], lm0).then_inc(msg_weights_in, 16)
            sp.dma_start(wa[64:128, 0:F1], wm011.rearrange("u a w -> u (a w)")).then_inc(msg_weights_in, 16)
            for k in range(3):
                sp.dma_start(wb[32 * k:32 * k + 32, 32 * k:32 * k + 32], lm1).then_inc(msg_weights_in, 16)
                sp.dma_start(wc[32 * k:32 * k + 32, 96 + 32 * k:128 + 32 * k],
                             wm101.rearrange("u a w -> u (a w)")).then_inc(msg_weights_in, 16)
            sp.dma_start(wc[96:128, F1:96], wm110.rearrange("u a w -> u (a w)")).then_inc(msg_weights_in, 16)
            for h in range(2):
                sp.dma_start(wtf[64 * h:64 * h + 64, 0:GB, :].rearrange("p c (i w) -> p (c i) w", w=F1),
                             wu101.rearrange("u v w -> v u w")).then_inc(weights_in, 16)
                sp.dma_start(wtf[64 * h:64 * h + 64, GB:2 * GB, :].rearrange("p c w -> p (c w)"),
                             wu011.rearrange("u v w -> u (v w)")).then_inc(weights_in, 16)
            by_chunk = wu000.rearrange("(c q b) v w -> q b v c w", q=2, b=2)
            for q in range(2):
                for b in range(2):
                    sp.dma_start(w000[64 * q:64 * q + 64, 16 * b:16 * b + 16, :], by_chunk[q, b, :, :, :]
                                 ).then_inc(weights_in, 16)
            sp.dma_start(w110[:, :, :], wu110.rearrange("u v w -> (u v) w").rearrange("(c p) w -> p c w", p=128)
                         ).then_inc(weights_in, 16)
            sp.dma_start(wl0[0:64, 0:64], lu0).then_inc(weights_in, 16)
            sp.dma_start(wl0[64:96, 64:96], lu1).then_inc(weights_in, 16)
            sp.dma_start(wl0[96:128, 96:128], lu1).then_inc(weights_in, 16)
            sp.dma_start(wl1[:, :], lu1).then_inc(weights_in, 16)

            def load_rows(t, first=False):
                if not first:
                    sp.wait_ge(same_made, t)
                sp.dma_start(rows[:, :, :], srcT_rows[t, :, :].rearrange("(a j) p -> a j p", a=1)
                             .to_broadcast((P, J, P))).then_inc(rows_in, 16)

            load_rows(0, first=True)
            sp.wait_ge(zeros_made, 1)
            with sp.Fori(0, NZERO // ZSTEP) as i:
                sp.wait_ge(made, i * len(PRODUCTS) + len(PRODUCTS))
                for n in range(ZSTEP):
                    sp.dma_start(acc[bass.ds((i * ZSTEP + n) * (P * ZR), P * ZR), :].rearrange(
                        "(p a r) c -> p a (r c)", p=P, r=2), zeros[:, :, :].to_broadcast((P, ZR // 2, 2 * C))
                        ).then_inc(acc_zeroed, 16)
            sp.dma_start(acc[N:N + DUMP, :], zeros[:, 0, 0:C]).then_inc(acc_zeroed, 16)
            with sp.Fori(1, TILES) as t:
                load_rows(t)

            def x_loads(n, b):
                sp.dma_start(xa[:, b, :], xT[0:128, bass.ds(n * TN, TN)]).then_inc(nx_in[b], 16)
                sp.dma_start(xb[:, b, :], xT[128:160, bass.ds(n * TN, TN)]).then_inc(nx_in[b], 16)

            def acc_load(n, b):
                sp.dma_start(ya[:, b, :], acc[bass.ds(n * TN, TN), :].rearrange("(p j) c -> p (j c)", p=P)
                             ).then_inc(na_in[b], 16)

            def node_store(n, b):
                sp.wait_ge(n_norm, n + 1)
                sp.dma_start(out[bass.ds(n * TN, TN), :].rearrange("(p j) c -> p (j c)", p=P), yo[:, b, :]
                             ).then_inc(n_out[b], 16)

            sp.wait_ge(a_used, TILES * GA)
            sp.wait_ge(bc_used, TILES * GB)
            for n in range(NB):
                x_loads(n, n)
            sp.wait_ge(scattered, 16 * J * TILES)
            for n in range(NB):
                acc_load(n, n)
            with sp.Fori(1, NT // NB) as i:
                for b in range(NB):
                    node_store(NB * i + (b - NB), b)
                    x_loads(NB * i + b, b)
                    acc_load(NB * i + b, b)
            for n in range(NT // NB * NB, NT):
                node_store(n - NB, n % NB)
                x_loads(n, n % NB)
                acc_load(n, n % NB)
            for n in range(NT - NB, NT):
                node_store(n, n % NB)
            for b in range(NB):
                sp.wait_ge(n_out[b], 16 * ((NT - b + NB - 1) // NB))

        @block.gpsimd
        def _(pool):
            pool.memset(wa[:, :], 0.0).then_inc(small_zeroed, 1)
            pool.memset(wb[:, :], 0.0).then_inc(small_zeroed, 1)
            pool.memset(wc[:, :], 0.0).then_inc(small_zeroed, 1)
            pool.memset(wl0[:, :], 0.0).then_inc(small_zeroed, 1)
            pool.memset(dst_all[:, COLS:COLS + J], 0.0)
            pool.memset(src_all[:, COLS:COLS + J], 0.0)
            pool.wait_ge(tables_in, 48)

            def gather_start(f, pos=None):
                if pos:
                    pool.wait_ge(xi_in, f * 64)
                    pool.wait_ge(xj_in, f * 64)
                pool.tensor_copy(dcur[:, :], dst_all[:, bass.ds(f * J, J)]).then_inc(idx_cur, 1)
                pool.tensor_copy(scur[:, :], src_all[:, bass.ds(f * J, J)]).then_inc(idx_cur, 1)
                pool.wait_ge(idx_cur, f * 2 + 2)
                if pos:
                    pool.wait_ge(aux_evac, pos.after("ft2"))
                    pool.wait_ge(rx_done, f)
                pool.sem_inc(parted, 1)

            def gather(j):
                pool.indirect_dma_start(G[:, j, F0:F0 + C], None, x,
                                        bass.IndirectOffsetOnAxis(ap=dcur[:, j:j + 1], axis=0)).then_inc(xj_in, 16)
                pool.indirect_dma_start(XI[:, j, :], None, x,
                                        bass.IndirectOffsetOnAxis(ap=scur[:, j:j + 1], axis=0)).then_inc(xi_in, 16)

            def remainder(out, whole, S, p, first=0):
                (o_s, o_v), (p_s, p_v) = out, part(S, p)
                pool.tensor_tensor(o_s, scalars(whole, first), p_s, ALU.subtract)
                return pool.tensor_tensor(o_v, vectors(whole, first), p_v, ALU.subtract)

            def rest_x(f, step):
                if step == 0:
                    pool.wait_ge(hx_done, f + 1)
                    remainder((scalars(R), vectors(R)), XI, SX, 0).then_inc(rx_done, 1)
                else:
                    pool.wait_ge(mx_done, f + 1)
                    remainder(part(SX, 2), R, SX, 1).then_inc(lx_done, 1)

            def rest_a(f, step):
                if step == 0:
                    pool.wait_ge(ha_done, f + 1)
                    remainder((scalars(R), vectors(R)), M, SA, 0, F1).then_inc(ra_done, 1)
                else:
                    pool.wait_ge(ma_done, f + 1)
                    remainder(part(SA, 2), R, SA, 1).then_inc(la_done, 1)

            def features(f):
                pool.wait_ge(xj_in, f * 64 + 64)
                pool.wait_ge(attr_cur, f + 1)
                e0 = acur[:, :, 3:4]
                pool.tensor_tensor(G[:, :, 0:F0], G[:, :, F0:2 * F0], e0.to_broadcast((P, J, F0)), ALU.mult
                                   ).then_inc(feat_pool, 1)
                pool.tensor_tensor(H[:, :, 0:96], G[:, :, 2 * F0:F0 + C], e0.to_broadcast((P, J, 96)), ALU.mult
                                   ).then_inc(feat_pool, 1)

            def scatter(b, j, pos, first=False):
                pool.wait_ge(aux_evac, pos.after(f"ud{j // 2}"))
                pool.wait_ge(sidx_made, b + 1)
                pool.wait_ge(acc_zeroed, 16 * (NZERO + 1))
                if not (first and j == 0):
                    pool.wait_ge(scattered, b * 64 + 16 * j)
                pool.sem_inc(parted, 1)
                pool.indirect_dma_start(acc, bass.IndirectOffsetOnAxis(ap=sidx[:, j:j + 1], axis=0), UL[:, j, :], None,
                                        compute_op=ALU.add).then_inc(scattered, 16)

            def body(t, par, back, front):
                pos = body_pos(t, par, back, front)

                def product(s, name):
                    pool.wait_ge(made, t * NV + v_after(s, name))

                def add_bc(s, k):
                    if k in ADDS[s]:
                        product(s, "C01" if k < 2 else "C2")
                        pool.tensor_tensor(ZB[:, s % 4, k, :], ZB[:, s % 4, k, :], ZC[:, s % 4, k, :], ALU.add
                                           ).then_inc(z_made, 1)

                for s in range(SLOTS):
                    if front and s == 0:
                        features(t + 1)
                    product(s, "P01")
                    if s >= 2 or back:
                        pool.wait_ge(bc_used, t * GB + (s - 1))
                    pool.tensor_tensor(QB[:, s % 2, :], PB[:, s % 2, 0, :], PB[:, s % 2, 1, :], ALU.add
                                       ).then_inc(q_half, 1)
                    add_bc(s, 0)
                    if front and s in (4, 5):
                        rest_a(t + 1, s - 4)
                    if back and s >= 6:
                        scatter(t - 1, 2 * (s - 6), pos, isinstance(t, int) and t == 1)
                    add_bc(s, 1)
                    product(s, "P2")
                    pool.wait_ge(q_half, t * GB + (s + 1))
                    pool.tensor_tensor(QB[:, s % 2, :], QB[:, s % 2, :], PB[:, s % 2, 2, :], ALU.add
                                       ).then_inc(q_made, 1)
                    add_bc(s, 2)
                    if front and s in (0, 1):
                        rest_x(t + 1, s)
                    if back and s >= 6:
                        scatter(t - 1, 2 * (s - 6) + 1, pos)
                    if front and GATHER_SLOT <= s < GATHER_SLOT + J:
                        if s == GATHER_SLOT:
                            gather_start(t + 2, pos)
                        gather(s - GATHER_SLOT)

            gather_start(0)
            for j in range(J):
                gather(j)
            features(0)
            rest_x(0, 0)
            rest_x(0, 1)
            gather_start(1, prologue_pos())
            for j in range(J):
                gather(j)
            rest_a(0, 0)
            rest_a(0, 1)
            body(0, 0, False, True)
            with pool.Fori(0, (TILES - 2) // 2) as i:
                body(2 * i + 1, 1, True, True)
                body(2 * i + 2, 0, True, True)
            body(TILES - 1, 1, True, False)
            tail = tail_pos()
            for j in range(J):
                scatter(TILES - 1, j, tail)
            pool.wait_ge(xj_in, 64 * (TILES + 1))
            pool.wait_ge(xi_in, 64 * (TILES + 1))

        @block.scalar
        def _(act):
            copy = ACT.Copy

            def scale(done, pairs_of_weights):
                for ap, s in pairs_of_weights:
                    act.activation(ap, ap, copy, scale=s).then_inc(done, 1)

            r96 = 96.0 ** -0.5

            def scale_message_weights():
                act.wait_ge(msg_weights_in, 16 * 10)
                scale(msg_weights_ready, ((wa[0:64, :], r96), (wa[64:128, F1:96], 0.125), (wa[64:128, 0:F1], r96),
                                          (wb[:, :], 32.0 ** -0.5), (wc[0:96, :], r96),
                                          (wc[96:128, :], (3.0 * 96.0) ** -0.5)))

            def scale_weights():
                act.wait_ge(weights_in, 16 * 13)
                scale(weights_ready, ((wtf, 1.0 / 64), (w000[:, :, :], 5120.0 ** -0.5),
                                      (w110[:, :, :], (3.0 * 5120.0) ** -0.5), (wl0[0:64, :], 0.125),
                                      (wl0[64:128, :], 32.0 ** -0.5), (wl1[:, :], 32.0 ** -0.5)))

            def split_w(step):
                if step == 0:
                    act.wait_ge(weights_ready, 1)
                    act.activation(wt[:, 0, :, :], wtf, copy).then_inc(wh_done, 1)
                    act.activation(wt[64:128, 2, :, :], wtf[64:128, :, :], copy).then_inc(wh_done, 1)
                else:
                    act.wait_ge(wr_done, 1)
                    act.activation(wt[:, 1, :, :], wtr, copy).then_inc(wm_done, 1)

            def evac(dst_ap, pos, name, ps):
                act.wait_ge(aux_ready, pos.after(name))
                act.activation(dst_ap, ps, copy).then_inc(aux_evac, 1)

            def bank(pos, name):
                return aux[pos.bank(name)]

            def front_piece(name, par, pos):
                ps = bank(pos, name)
                n = int(name[-1])
                if name.startswith("ft"):
                    r = 96 if n == 1 else 128
                    evac(FT[0:r, n, :], pos, name, ps[0:r, 0:T])
                elif name.startswith("m"):
                    evac(M[:, n, :], pos, name, ps[0:P, 0:C + F1])
                elif name.startswith("v"):
                    evac(V[:, par, n, :], pos, name, ps[:, 0:T])
                elif name.startswith("sx"):
                    evac(ST[:, par, n, :], pos, name, ps[0:96, 0:T])
                elif name.startswith("sa"):
                    evac(ST[:, par, 5 + n, :], pos, name, ps[0:96, 0:T])
                else:
                    evac(REP[:, par, n, :], pos, name, ps[:, 0:T])

            def round_to(S, p, whole, first=0):
                p_s, p_v = part(S, p)
                act.activation(p_s, scalars(whole, first), copy)
                return act.activation(p_v, vectors(whole, first), copy)

            def split_x(f, step):
                if step == 0:
                    act.wait_ge(xi_in, (f + 1) * 64)
                    round_to(SX, 0, XI).then_inc(hx_done, 1)
                else:
                    act.wait_ge(rx_done, f + 1)
                    round_to(SX, 1, R).then_inc(mx_done, 1)

            def split_a(f, step):
                if step == 0:
                    act.wait_ge(msg_done, f + 1)
                    round_to(SA, 0, M, F1).then_inc(ha_done, 1)
                else:
                    act.wait_ge(ra_done, f + 1)
                    round_to(SA, 1, R).then_inc(ma_done, 1)

            def acc_out(b):
                act.wait_ge(bc_used, (b + 1) * GB)
                act.wait_ge(a_used, (b + 1) * GA)
                act.activation(U0[:, :], acc0[:, 0:T], copy).then_inc(acc_evac, 1)
                act.activation(U1[:, :], acc1[0:96, 0:T], copy).then_inc(acc_evac, 1)

            def back_piece(name, b, pos, first=False):
                n = int(name[-1])
                if name == "ul0" and not first:
                    act.wait_ge(scattered, b * 64)
                evac(UL[:, 2 * n:2 * n + 2, :], pos, name,
                     bank(pos, name)[0:P, 0:2 * C].rearrange("p (j c) -> p j c", j=2))

            def body(t, par, back, front):
                pos = body_pos(t, par, back, front)

                def pieces(s, point):
                    if back:
                        for name in BACK_AT.get((s, point), []):
                            back_piece(name, t - 1, pos, isinstance(t, int) and t == 1)
                    if front:
                        for name in FRONT_AT.get((s, point), []):
                            front_piece(name, 1 - par, pos)

                for s in range(SLOTS):
                    for point in range(5):
                        for name in T_AT.get((s, point), []):
                            u = int(name[-1])
                            if u >= 2:
                                act.wait_ge(made, t * NV + v_after(u - 2, "C2"))
                            evac(TS[:, 2 * (u % 2) + (name[1] == "0"), :], pos, name, bank(pos, name)[:, 0:T])
                        pieces(s, point)
                        if front and (s, point) in ((0, 0), (1, 1)):
                            split_x(t + 1, s)
                        if front and (s, point) in ((4, 1), (5, 0)):
                            split_a(t + 1, s - 4)
                        if back and (s, point) == (0, 3):
                            acc_out(t - 1)

            pro = prologue_pos()
            split_x(0, 0)
            split_x(0, 1)
            scale_message_weights()
            for name in FRONT:
                if name == "v2":
                    split_a(0, 0)
                    split_a(0, 1)
                    scale_weights()
                    split_w(0)
                front_piece(name, 0, pro)
            split_w(1)
            body(0, 0, False, True)
            with act.Fori(0, (TILES - 2) // 2) as i:
                body(2 * i + 1, 1, True, True)
                body(2 * i + 2, 0, True, True)
            body(TILES - 1, 1, True, False)
            tail = tail_pos()
            acc_out(TILES - 1)
            for name in ("ul0", "ul1", "ud0", "ud1"):
                back_piece(name, TILES - 1, tail)

            def node_sd(n, b):
                act.wait_ge(n_mv, n + 1)
                act.activation(sd[:, b, :], ve[:, b, :], ACT.Sqrt).then_inc(n_sd, 1)

            def node_norm(n, b, left):
                act.wait_ge(n_rs, n + 1)
                if left is not None:
                    act.wait_ge(n_out[b], left * 16)
                for j in range(JN):
                    last = act.activation(yo[:, b, j * C:(j + 1) * C], ya[:, b, j * C:(j + 1) * C], ACT.Identity,
                                          bias=nb[:, b, j:j + 1], scale=rs[:, b, j:j + 1])
                last.then_inc(n_norm, 1)

            node_sd(0, 0)
            for n in range(NB):
                node_sd(n + 1, (n + 1) % NB)
                node_norm(n, n, None)
            with act.Fori(1, NT // NB) as i:
                for b in range(NB):
                    node_sd(NB * i + (b + 1), (b + 1) % NB)
                    node_norm(NB * i + b, b, i)
            for n in range(NT // NB * NB, NT):
                if n + 1 < NT:
                    node_sd(n + 1, (n + 1) % NB)
                node_norm(n, n % NB, n // NB)

        @block.vector
        def _(dve):
            def load_attr(f, first=False):
                if not first:
                    dve.wait_ge(feat_pool, f * 2)
                dve.tensor_copy(acur[:, :, :].rearrange("p j a -> p (j a)"), attr_all[:, bass.ds(f * (4 * J), 4 * J)]
                                ).then_inc(attr_cur, 1)

            def dot_r(f):
                dve.wait_ge(xj_in, (f + 1) * 64)
                dve.wait_ge(attr_cur, f + 1)
                r = acur[:, :, 0:3].rearrange("p j (k a) -> p j k a", a=1).to_broadcast((P, J, 3, F1))
                dve.tensor_tensor(rx1, G[:, :, 2 * F0:F0 + C].rearrange("p j (k u) -> p j k u", k=3), r,
                                  ALU.mult).then_inc(rx1_made, 1)
                dve.wait_ge(rx1_made, f + 1)
                dve.tensor_reduce(H[:, :, 96:128], rx1.rearrange("p j k u -> p j u k"), AX.X, ALU.add
                                  ).then_inc(feat_dve, 1)

            def message(f, pos):
                dve.wait_ge(aux_evac, pos.after("m3"))
                z = M[:, :, 0:F1].rearrange("p j (a w) -> p j a w", a=1).to_broadcast((P, J, 3, F1))
                r = acur[:, :, 0:3].rearrange("p j (k a) -> p j k a", a=1).to_broadcast((P, J, 3, F1))
                dve.tensor_tensor(rx1, z, r, ALU.mult).then_inc(rz_made, 1)
                dve.wait_ge(rz_made, f + 1)
                a1 = M[:, :, F1 + F0:F1 + C]
                dve.tensor_tensor(a1, a1, rx1.rearrange("p j k w -> p j (k w)"), ALU.add
                                  ).then_inc(msg_done, 1)

            def repeats(b, step, first=False):
                if step == 0:
                    dve.tensor_copy(srcf[:, :], src_all[:, bass.ds(b * J, J)]).then_inc(srcf_made, 1)
                    dve.wait_ge(srcf_made, b + 1)
                    dve.wait_ge(rows_in, (b + 1) * 16)
                    dve.tensor_tensor(same[:, :, :], rows[:, :, :],
                                      srcf[:, :].rearrange("p (j a) -> p j a", a=1).to_broadcast((P, J, P)),
                                      ALU.is_equal).then_inc(same_made, 1)
                elif step == 1:
                    dve.wait_ge(same_made, b + 1)
                    dve.tensor_tensor(prior, same[:, :, :],
                                      earlier[:, :].rearrange("p (a e) -> p a e", a=1).to_broadcast((P, J, P)),
                                      ALU.mult).then_inc(prior_made, 1)
                    dve.wait_ge(prior_made, b + 1)
                    dve.tensor_reduce(dup[:, :], prior, AX.X, ALU.add).then_inc(idx_step, 1)
                else:
                    dve.tensor_scalar(todump[:, :], srcf[:, :], -1.0, dump[:, 0:1], ALU.mult, ALU.add
                                      ).then_inc(idx_step, 1)
                    dve.wait_ge(idx_step, b * 4 + 2)
                    dve.tensor_scalar(dup[:, :], dup[:, :], 1.0, None, ALU.min).then_inc(idx_step, 1)
                    dve.wait_ge(idx_step, b * 4 + 3)
                    dve.tensor_tensor(todump[:, :], todump[:, :], dup[:, :], ALU.mult).then_inc(idx_step, 1)
                    dve.wait_ge(idx_step, b * 4 + 4)
                    if not first:
                        dve.wait_ge(scattered, b * 64)
                    dve.tensor_tensor(sidx[:, :], todump[:, :], srcf[:, :], ALU.add).then_inc(sidx_made, 1)

            def body(t, par, back, front):
                pos = body_pos(t, par, back, front)
                def replicated(n):
                    if isinstance(t, int) and t == 0:
                        dve.wait_ge(aux_evac, len(FRONT) - n)
                    else:
                        dve.wait_ge(aux_evac, pos.start() - n)


                def copied_in(s, name):
                    n = copy_use(s, name)
                    dve.wait_ge(copied, t * NX + (n + 1))
                    return 2 * (n % 2)

                def twice(a):
                    return a.rearrange("p (a e) -> p a e", a=1).to_broadcast((128, 2, T))

                def multiply(o, i0, i1):
                    dve.tensor_tensor(o, i0, i1, ALU.mult).then_inc(made, 1)

                for s in range(SLOTS):
                    h, z = s % 2, s % 4
                    t101, t011 = TS[:, 2 * h, :], TS[:, 2 * h + 1, :]
                    if s >= 2 or back:
                        dve.wait_ge(a_used, t * GA + (s - 1))
                    if s == 0:
                        replicated(3)
                    b = copied_in(s, "A01")
                    multiply(PA[:, 4 * h:4 * h + 2, :], copies[:, b:b + 2, 0:T], twice(REP[:, par, 0, :]))
                    if front:
                        f = t + 1
                        if s == 0:
                            load_attr(f)
                            dot_r(f)
                    if s >= 2 or back:
                        dve.wait_ge(q_made, t * GB + (s - 1))
                    if s == 0:
                        replicated(1)
                    b = copied_in(s, "X01")
                    multiply(PB[:, h, 0:2, :], copies[:, b:b + 2, 0:T], REP[:, par, 1:3, :])
                    dve.wait_ge(aux_evac, pos.after(f"t101_{s}"))
                    if s >= 4 or back:
                        dve.wait_ge(bc_used, t * GB + (s - 3))
                    multiply(ZB[:, z, 0:2, :], copies[:, b:b + 2, 0:T], twice(t101))
                    dve.wait_ge(aux_evac, pos.after(f"t011_{s}"))
                    if front and s == 3:
                        message(f, pos)
                    b = copied_in(s, "V01")
                    multiply(ZC[:, z, 0:2, :], copies[:, b:b + 2, 0:T], twice(t011))
                    b = copied_in(s, "A23")
                    multiply(PA[:, 4 * h + 2:4 * h + 4, :], copies[:, b:b + 2, 0:T], twice(REP[:, par, 0, :]))
                    if s == 0:
                        replicated(0)
                    b = copied_in(s, "XV2")
                    multiply(PB[:, h, 2, :], copies[:, b, 0:T], REP[:, par, 3, :])
                    multiply(ZB[:, z, 2, :], copies[:, b, 0:T], t101)
                    multiply(ZC[:, z, 2, :], copies[:, b + 1, 0:T], t011)
                    if back and 2 <= s < 5:
                        repeats(t - 1, s - 2, isinstance(t, int) and t == 1)

            dve.memset(zeros[:, :, :], 0.0).then_inc(zeros_made, 1)
            dve.wait_ge(tables_in, 48)
            pro = prologue_pos()
            load_attr(0, first=True)
            dot_r(0)
            message(0, pro)
            dve.wait_ge(wh_done, 2)
            dve.tensor_tensor(wtr, wtf, wt[:, 0, :, :], ALU.subtract).then_inc(wr_done, 1)
            dve.wait_ge(wm_done, 1)
            dve.tensor_tensor(wt[0:64, 2, :, :], wtr[0:64, :, :], wt[0:64, 1, :, :], ALU.subtract).then_inc(wl_done, 1)
            body(0, 0, False, True)
            with dve.Fori(0, (TILES - 2) // 2) as i:
                body(2 * i + 1, 1, True, True)
                body(2 * i + 2, 0, True, True)
            body(TILES - 1, 1, True, False)
            for step in range(3):
                repeats(TILES - 1, step)

            dve.wait_ge(weights_ready, NSCALE)
            dve.wait_ge(consts_in, NCONST)
            dve.scalar_tensor_tensor(wl0[:, :], eye[:, :], 2.0, wl0[:, :], ALU.mult, ALU.add).then_inc(wl_ready, 1)
            dve.scalar_tensor_tensor(wl1[:, :], eye[0:32, 0:32], 2.0, wl1[:, :], ALU.mult, ALU.add
                                     ).then_inc(wl_ready, 1)

            def node_stats(n, b, group):
                dve.wait_ge(n_lin, n + 1)
                dve.wait_ge(na_in[b], (group + 1) * 16)
                y = ya[:, b, :].rearrange("p (q c) -> p q c", q=4)
                dve.tensor_tensor(y, quads[b % 2][0:P, :, 0:2 * C], y, ALU.add).then_inc(n_sum, 1)
                dve.wait_ge(n_sum, n + 1)
                for j in range(JN):
                    last = dve.bn_stats(stats[:, b, j, :], ya[:, b, j * C:(j + 1) * C])
                last.then_inc(n_stats, 1)
                dve.wait_ge(n_stats, n + 1)
                dve.sem_inc(parted_v, 1)
                for j in range(JN):
                    last = dve.bn_aggr(mv[:, b, j, :], stats[:, b, j, :])
                last.then_inc(n_aggr, 1)
                dve.wait_ge(n_aggr, n + 1)
                dve.tensor_scalar(ve[:, b, :], mv[:, b, :, 1], EPS, None, ALU.add).then_inc(n_mv, 1)

            def node_scale(n, b):
                dve.wait_ge(n_sd, n + 1)
                dve.reciprocal(r0[:, b, :], sd[:, b, :]).then_inc(n_step, 1)
                dve.wait_ge(n_step, n * 4 + 1)
                dve.tensor_tensor(hv[:, b, :], r0[:, b, :], r0[:, b, :], ALU.mult).then_inc(n_step, 1)
                dve.wait_ge(n_step, n * 4 + 2)
                dve.tensor_tensor(hv[:, b, :], hv[:, b, :], ve[:, b, :], ALU.mult).then_inc(n_step, 1)
                dve.wait_ge(n_step, n * 4 + 3)
                dve.tensor_scalar(hv[:, b, :], hv[:, b, :], -0.5, 1.5, ALU.mult, ALU.add).then_inc(n_step, 1)
                dve.wait_ge(n_step, n * 4 + 4)
                dve.tensor_tensor(rs[:, b, :], r0[:, b, :], hv[:, b, :], ALU.mult).then_inc(n_rs0, 1)
                dve.wait_ge(n_rs0, n + 1)
                dve.scalar_tensor_tensor(nb[:, b, :], mv[:, b, :, 0], -1.0, rs[:, b, :], ALU.mult, ALU.mult
                                         ).then_inc(n_rs, 1)

            for n in range(NB):
                node_stats(n, n, 0)
                if n:
                    node_scale(n - 1, n - 1)
            with dve.Fori(1, NT // NB) as i:
                for b in range(NB):
                    node_stats(NB * i + b, b, i)
                    node_scale(NB * i + (b - 1), (b - 1) % NB)
            for n in range(NT // NB * NB, NT):
                node_stats(n, n % NB, n // NB)
                node_scale(n - 1, (n - 1) % NB)
            node_scale(NT - 1, (NT - 1) % NB)

        @block.tensor
        def _(pe):
            def aux_bank(pos, name):
                after = pos.after(name)
                if not (isinstance(after, int) and after <= 2):
                    pe.wait_ge(aux_evac, after - 2)
                return aux[pos.bank(name)]

            def front_piece(name, f, par, pos):
                n = int(name[-1])
                if name == "ft0":
                    pe.wait_ge(feat_pool, f * 2 + 2)
                    pe.wait_ge(feat_dve, f + 1)
                elif name == "m0":
                    pe.wait_ge(aux_evac, pos.after("ft2"))
                    if isinstance(f, int) and f == 0:
                        pe.wait_ge(msg_weights_ready, 6)
                elif name == "sx0":
                    pe.wait_ge(lx_done, f + 1)
                elif name == "v2":
                    pe.wait_ge(la_done, f + 1)
                elif name == "rep0":
                    pe.wait_ge(aux_evac, pos.after("sa4"))
                ps = aux_bank(pos, name)
                if name.startswith("ft"):
                    for j in range(J):
                        f_in = (G[:, j, 0:128], G[:, j, 128:224], H[:, j, :])[n]
                        m = 96 if n == 1 else 128
                        last = pe.transpose(ps[0:m, j * P:(j + 1) * P], f_in, eye[0:P, 0:P])
                elif name.startswith("m"):
                    e = slice(n * P, (n + 1) * P)
                    pe.matmul(ps[0:P, 0:96], FT[:, 0, e], wa[:, :], start=True, stop=False)
                    pe.matmul(ps[0:P, 0:96], FT[:, 2, e], wc[:, 0:96], start=False, stop=True)
                    pe.matmul(ps[0:P, 96:192], FT[0:96, 1, e], wb[:, :], start=True, stop=False)
                    last = pe.matmul(ps[0:P, 96:192], FT[:, 2, e], wc[:, 96:192], start=False, stop=True)
                elif name.startswith("v"):
                    S = (SX, SA)[n // 2]
                    o = F0 * (n % 2)
                    for j in range(J):
                        last = pe.matmul(ps[:, j * P:(j + 1) * P], S[:, j, o:o + 2 * F0], eyeb[0:P, 0:P], start=True, stop=True)
                elif name.startswith("s"):
                    S = SX if name[1] == "x" else SA
                    stack = slice(n, 3 * F0, 2) if n < 2 else slice(96 * n, 96 * n + 96)
                    for j in range(J):
                        last = pe.matmul(ps[0:96, j * P:(j + 1) * P], S[:, j, stack],
                                         eyeb[0:P, 0:P], start=True, stop=True)
                elif n == 0:
                    for b in range(2):
                        last = pe.matmul(ps[:, 0:T], sel[:, REPA + b, :], ST[:, par, 5 + b, :],
                                         start=(b == 0), stop=(b == 1))
                else:
                    last = pe.matmul(ps[:, 0:T], sel[:, REP4, :], ST[:, par, 6 + n, :], start=True, stop=True)
                last.then_inc(aux_ready, 1)

            def back_piece(name, b, pos):
                n = int(name[-1])
                if name == "ul0":
                    pe.wait_ge(acc_evac, b * 2 + 2)
                elif name == "ud0":
                    pe.wait_ge(same_made, b + 1)
                    pe.wait_ge(aux_evac, pos.after("ul1"))
                ps = aux_bank(pos, name)
                for jj in range(2):
                    j, o = 2 * n + jj, jj * C
                    if name[1] == "l":
                        pe.matmul(ps[0:P, o:o + F0], U0[:, j * P:(j + 1) * P], fold[:, :], start=True, stop=True)
                        last = pe.transpose(ps[0:P, o + F0:o + C], U1[:, j * P:(j + 1) * P], eye[0:96, 0:96])
                    else:
                        last = pe.matmul(ps[0:P, o:o + C], same[:, j, :], UL[:, j, :], start=True, stop=True)
                last.then_inc(aux_ready, 1)

            def copy_pair(t, par, back, s, name):
                n = copy_use(s, name)
                if n >= 2:
                    q, r = divmod(n - 2, len(COPIES))
                    pe.wait_ge(made, t * NV + v_after(q, FREES[COPIES[r]]))
                elif back:
                    pe.wait_ge(made, t * NV + (v_after(SLOTS - 1, FREES[COPIES[n - 2]]) - NV))
                for i in range(2):
                    if name[0] == "A":
                        c = 4 * s + int(name[1]) + i
                        lhsT, rhs = sel[:, SEL2 + c % 16, :], ST[:, par, c // 16, :]
                    else:
                        stack = {"X01": 2 + i, "V01": 7 + i, "XV2": 4 + 5 * i}[name]
                        lhsT, rhs = sel[:, SEL4 + s, :], ST[:, par, stack, :]
                    last = pe.matmul(copies[:, 2 * (n % 2) + i, 0:T], lhsT, rhs, start=True, stop=True)
                last.then_inc(copied, 1)

            def contract_a(t, s, pair):
                pe.wait_ge(made, t * NV + v_after(s, ("A01", "A23")[pair]))
                for i in (2 * pair, 2 * pair + 1):
                    c = 4 * s + i
                    h = 64 * (c % 2)
                    last = pe.matmul(acc0[h:h + 64, 0:T], w000[:, c, :], PA[:, c % 8, :],
                                     start=(c < 2), stop=(c >= NA - 2))
                if pair:
                    last.then_inc(a_used, 1)

            def contract_bc(t, s):
                h = 64 * (s % 2)
                pe.wait_ge(q_made, t * GB + (s + 1))
                pe.matmul(acc0[h:h + 64, 0:T], w110[:, s, :], QB[:, s % 2, :], start=False, stop=False)
                for k in range(3):
                    o, stop = acc1[32 * k:32 * k + 32, 0:T], s == SLOTS - 1
                    if k in ADDS[s]:
                        pe.wait_ge(z_made, t * NZ + z_after(s, k))
                    else:
                        pe.wait_ge(made, t * NV + v_after(s, "C2"))
                        pe.matmul(o, sum4[:, :], ZC[:, s % 4, k, :], start=(s == 0), stop=False)
                    last = pe.matmul(o, sum4[:, :], ZB[:, s % 4, k, :], start=(s == 0 and k in ADDS[s]), stop=stop)
                last.then_inc(bc_used, 1)

            def body(t, par, back, front):
                pos = body_pos(t, par, back, front)
                if isinstance(t, int) and t == 0:
                    pe.wait_ge(aux_evac, prologue_pos().after("sa4"))
                else:
                    pe.wait_ge(aux_evac, pos.start() - 4)
                assert FRONT[-5] == "sa4"

                def pieces(s, point):
                    for name in T_AT.get((s, point), []):
                        w = int(name[-1]) + (GB if name[1] == "0" else 0)
                        ps = aux_bank(pos, name)
                        x_or_a = 2 if w < GB else 0
                        for n, v in ((0, 0), (1, 0), (2, 1)):
                            last = pe.matmul(ps[:, 0:T], wt[:, n, w, :], V[:, par, x_or_a + v, :],
                                             start=(n == 0), stop=(n == 2))
                        last.then_inc(aux_ready, 1)
                    if back:
                        for name in BACK_AT.get((s, point), []):
                            back_piece(name, t - 1, pos)
                    if front:
                        for name in FRONT_AT.get((s, point), []):
                            front_piece(name, t + 1, 1 - par, pos)


                for s in range(SLOTS):
                    u, v = (t, s - 1) if s else (t - 1, SLOTS - 1)
                    lagging = s > 0 or back

                    copy_pair(t, par, back, s, "A01")
                    pieces(s, 0)
                    copy_pair(t, par, back, s, "X01")
                    if s == 1 and back:
                        pe.wait_ge(acc_evac, t * 2)
                    if lagging:
                        contract_a(u, v, 0)
                    pieces(s, 1)
                    copy_pair(t, par, back, s, "V01")
                    if lagging:
                        contract_bc(u, v)
                    pieces(s, 2)
                    copy_pair(t, par, back, s, "A23")
                    if lagging:
                        contract_a(u, v, 1)
                    pieces(s, 3)
                    copy_pair(t, par, back, s, "XV2")
                    pieces(s, 4)

            pe.wait_ge(consts_in, NCONST)
            pro = prologue_pos()
            for name in FRONT:
                front_piece(name, 0, 0, pro)
            pe.wait_ge(weights_ready, NSCALE)
            pe.wait_ge(wh_done, 2)
            pe.wait_ge(wm_done, 1)
            pe.wait_ge(wl_done, 1)
            body(0, 0, False, True)
            with pe.Fori(0, (TILES - 2) // 2) as i:
                body(2 * i + 1, 1, True, True)
                body(2 * i + 2, 0, True, True)
            body(TILES - 1, 1, True, False)
            contract_a(TILES - 1, SLOTS - 1, 0)
            contract_bc(TILES - 1, SLOTS - 1)
            contract_a(TILES - 1, SLOTS - 1, 1)
            tail = tail_pos()
            for name in ("ul0", "ul1", "ud0", "ud1"):
                back_piece(name, TILES - 1, tail)

            pe.wait_ge(wl_ready, 2)

            pe.wait_ge(aux_evac, tail.after("ud1"))

            def node_lin(n, b, group, reuse):
                if reuse:
                    pe.wait_ge(n_sum, n - 1)
                pe.wait_ge(nx_in[b], (group + 1) * 32)
                for j in range(JN):
                    ps = quads[b % 2][0:P, j // 2, (j % 2) * C:(j % 2 + 1) * C]
                    pe.matmul(ps[:, 0:128], xa[:, b, j * P:(j + 1) * P], wl0[:, :], start=True, stop=True)
                    last = pe.matmul(ps[:, 128:C], xb[:, b, j * P:(j + 1) * P], wl1[:, :], start=True, stop=True)
                last.then_inc(n_lin, 1)

            for n in range(NB):
                node_lin(n, n, 0, n >= 2)
            with pe.Fori(1, NT // NB) as i:
                for b in range(NB):
                    node_lin(NB * i + b, b, i, True)
            for n in range(NT // NB * NB, NT):
                node_lin(n, n % NB, n // NB, True)


_INS = ["x", "xT", "src", "srcT", "dst", "attr", "wm000", "wm011", "wm101", "wm110", "lm0", "lm1",
        "wu000", "wu011", "wu101", "wu110", "lu0", "lu1", "c_sel", "c_eyeb", "c_eye", "c_fold", "c_sum4",
        "c_earlier", "c_dump"]


def kernel(x, src, dst, edge_attr_4, node_vec1, **w):
    import ml_dtypes
    import concourse.bacc as _bacc
    from concourse.bass_utils import run_bass_kernel_spmd as _run

    x = np.asarray(x)
    xk = np.concatenate([x[:, :F0], x[:, F0:].reshape(N, F1, 3).transpose(0, 2, 1).reshape(N, 3 * F1)], 1)
    xT = xk.reshape(NT, P, JN, C).transpose(3, 0, 2, 1).reshape(C, N)
    arrays = {
        "x": xk, "xT": xT,
        "src": np.asarray(src).reshape(P, COLS), "srcT": np.asarray(src).reshape(P, COLS).T,
        "dst": np.asarray(dst).reshape(P, COLS), "attr": np.asarray(edge_attr_4).reshape(P, COLS * 4),
    }
    for name in _INS[6:18]:
        key = "L0_gnn_" + name
        arrays[name] = np.asarray(w[key])
    for name, (a, dt) in constants().items():
        arrays[name] = np.asarray(a, dtype=ml_dtypes.bfloat16 if dt == "bfloat16" else dt)
    arrays = {k + "_dram": np.ascontiguousarray(v) for k, v in arrays.items()}

    nc = _bacc.Bacc("TRN2", target_bir_lowering=False, num_devices=1)
    args = [nc.dram_tensor(n + "_dram", arrays[n + "_dram"].shape, mybir.dt.from_np(arrays[n + "_dram"].dtype),
                           kind="ExternalInput").ap() for n in _INS]
    out = nc.dram_tensor("out_dram", (N, C), mybir.dt.float32, kind="ExternalOutput").ap()
    build(nc, *args, out)
    got = _run(nc, [arrays], core_ids=[0]).results[0]["out_dram"]
    return np.concatenate([got[:, :F0], got[:, F0:].reshape(N, 3, F1).transpose(0, 2, 1).reshape(N, 3 * F1)], 1)
```
